# Optimizing a Trainium2 kernel written in Bass

```python
import numpy as np
import jax
import jax.numpy as jnp

def _softmax(x, axis=-1):
    return jax.nn.softmax(x, axis=axis)

def _gelu(x):
    return jax.nn.gelu(x, approximate=True)

def _silu(x):
    return jax.nn.silu(x)

def _sigmoid(x):
    return jax.nn.sigmoid(x)

def _layernorm(x, axis=-1, eps=1e-05):
    m = jnp.mean(x, axis=axis, keepdims=True)
    v = jnp.var(x, axis=axis, keepdims=True)
    return (x - m) / jnp.sqrt(v + eps)

def _scatter_add(tgt, idx, src, axis=0):
    return tgt.at[idx].add(src)

def _segment_sum(src, seg, n):
    return jax.ops.segment_sum(src, seg, n)
kernel_name = 'mk_audio_tower_d1_tok_audfeat256_r4_a49ae5'

def setup_inputs(seed: int=0):
    np.random.seed(seed)
    _w = jnp.asarray

    def _rec_inputs():
        import jax
        import jax.numpy as jnp
        _rk = jax.random.key(seed)
        x = jax.random.uniform(jax.random.fold_in(_rk, 1), (32, 4, 250), jnp.float32, 0.0, 0.999986)
        return x
    x = _rec_inputs()

    def _L0_tok_setup():
        import jax, jax.numpy as jnp
        import numpy as np
        T = 8
        key = jax.random.key(seed)
        ks = jax.random.split(key, 9)
        bs, dims, L, d = (16, 4, 512, 64)
        x = jax.random.uniform(ks[0], (bs, dims, L), dtype=jnp.float32)
        s_in = 1.0 / np.sqrt(dims)
        s_d = 1.0 / np.sqrt(d)
        W1 = jax.random.uniform(ks[1], (d, dims), minval=-s_in, maxval=s_in, dtype=jnp.float32)
        b1 = jax.random.uniform(ks[2], (d,), minval=-s_in, maxval=s_in, dtype=jnp.float32)
        W2 = jax.random.uniform(ks[3], (d, d), minval=-s_d, maxval=s_d, dtype=jnp.float32)
        b2 = jax.random.uniform(ks[4], (d,), minval=-s_d, maxval=s_d, dtype=jnp.float32)
        W3 = jax.random.uniform(ks[5], (d, dims), minval=-s_in, maxval=s_in, dtype=jnp.float32)
        b3 = jax.random.uniform(ks[6], (d,), minval=-s_in, maxval=s_in, dtype=jnp.float32)
        W4 = jax.random.uniform(ks[7], (d, d), minval=-s_d, maxval=s_d, dtype=jnp.float32)
        b4 = jax.random.uniform(ks[8], (d,), minval=-s_d, maxval=s_d, dtype=jnp.float32)
        return dict(x=x, W1=W1, b1=b1, W2=W2, b2=b2, W3=W3, b3=b3, W4=W4, b4=b4)
    _L0_tok_all = _L0_tok_setup()
    _L0_tok_in = {k: v for k, v in _L0_tok_all.items() if k in ('W1', 'b1', 'W2', 'b2', 'W3', 'b3', 'W4', 'b4')}
    del _L0_tok_all

    def _L0_attn_setup():
        import jax, jax.numpy as jnp
        import numpy as np
        EPS = 1e-05

        def _ln(x, scale):
            mu = jnp.mean(x, axis=-1, keepdims=True)
            var = jnp.var(x, axis=-1, keepdims=True)
            return (x - mu) / jnp.sqrt(var + EPS) * scale
        key = jax.random.key(seed)
        k = jax.random.split(key, 8)
        B, S, E, H = (4, 512, 64, 8)
        n_layer = 12
        x = jax.random.normal(k[0], (B, S, E), dtype=jnp.float32)
        e = jax.random.normal(k[1], (B, S, E), dtype=jnp.float32)
        p = jax.random.normal(k[2], (S, E), dtype=jnp.float32)
        W_q = 0.02 * jax.random.normal(k[3], (H, E, E), dtype=jnp.float32)
        W_k = 0.02 * jax.random.normal(k[4], (H, E, E), dtype=jnp.float32)
        W_v = 0.02 * jax.random.normal(k[5], (H, E, E), dtype=jnp.float32)
        W_o = 0.02 / np.sqrt(2 * n_layer) * jax.random.normal(k[6], (E, H * E), dtype=jnp.float32)
        gamma = jnp.ones((1, H, 1, 1), dtype=jnp.float32)
        ln_scale = jnp.ones((E,), dtype=jnp.float32)
        return {'x': x, 'e': e, 'p': p, 'ln_scale': ln_scale, 'W_q': W_q, 'W_k': W_k, 'W_v': W_v, 'W_o': W_o, 'gamma': gamma}
    _L0_attn_all = _L0_attn_setup()
    _L0_attn_in = {k: v for k, v in _L0_attn_all.items() if k in ('e', 'p', 'ln_scale', 'W_q', 'W_k', 'W_v', 'W_o', 'gamma')}
    del _L0_attn_all

    def _L0_ffn_setup():
        import jax, jax.numpy as jnp
        import numpy as np
        B, S, H, F, E, K = (8, 1024, 64, 128, 16, 2)
        EPS = 1e-05
        key = jax.random.key(seed)
        ks = jax.random.split(key, 9)
        sc = 0.02
        return {'x': jax.random.normal(ks[0], (B, S, H), dtype=jnp.float32), 'gate_w': jax.random.normal(ks[1], (H, E), dtype=jnp.float32) * sc, 'gate_b': jnp.zeros((E,), dtype=jnp.float32), 'w1': jax.random.normal(ks[2], (E, H, F), dtype=jnp.float32) * sc, 'b1': jnp.zeros((E, F), dtype=jnp.float32), 'w2': jax.random.normal(ks[3], (E, F, H), dtype=jnp.float32) * sc, 'b2': jnp.zeros((E, H), dtype=jnp.float32), 'gamma': jnp.ones((H,), dtype=jnp.float32), 'beta': jnp.zeros((H,), dtype=jnp.float32)}
    _L0_ffn_all = _L0_ffn_setup()
    _L0_ffn_in = {k: v for k, v in _L0_ffn_all.items() if k in ('gate_w', 'gate_b', 'w1', 'b1', 'w2', 'b2', 'gamma', 'beta')}
    del _L0_ffn_all
    return {'x': x, 'L0_tok_W1': _L0_tok_in['W1'], 'L0_tok_b1': _L0_tok_in['b1'], 'L0_tok_W2': _L0_tok_in['W2'], 'L0_tok_b2': _L0_tok_in['b2'], 'L0_tok_W3': _L0_tok_in['W3'], 'L0_tok_b3': _L0_tok_in['b3'], 'L0_tok_W4': _L0_tok_in['W4'], 'L0_tok_b4': _L0_tok_in['b4'], 'L0_attn_e': _L0_attn_in['e'], 'L0_attn_p': _L0_attn_in['p'], 'L0_attn_ln_scale': _L0_attn_in['ln_scale'], 'L0_attn_W_q': _L0_attn_in['W_q'], 'L0_attn_W_k': _L0_attn_in['W_k'], 'L0_attn_W_v': _L0_attn_in['W_v'], 'L0_attn_W_o': _L0_attn_in['W_o'], 'L0_attn_gamma': _L0_attn_in['gamma'], 'L0_ffn_gate_w': _L0_ffn_in['gate_w'], 'L0_ffn_gate_b': _L0_ffn_in['gate_b'], 'L0_ffn_w1': _L0_ffn_in['w1'], 'L0_ffn_b1': _L0_ffn_in['b1'], 'L0_ffn_w2': _L0_ffn_in['w2'], 'L0_ffn_b2': _L0_ffn_in['b2'], 'L0_ffn_gamma': _L0_ffn_in['gamma'], 'L0_ffn_beta': _L0_ffn_in['beta']}

def reference(x, L0_tok_W1, L0_tok_b1, L0_tok_W2, L0_tok_b2, L0_tok_W3, L0_tok_b3, L0_tok_W4, L0_tok_b4, L0_attn_e, L0_attn_p, L0_attn_ln_scale, L0_attn_W_q, L0_attn_W_k, L0_attn_W_v, L0_attn_W_o, L0_attn_gamma, L0_ffn_gate_w, L0_ffn_gate_b, L0_ffn_w1, L0_ffn_b1, L0_ffn_w2, L0_ffn_b2, L0_ffn_gamma, L0_ffn_beta):
    import jax
    import jax.numpy as jnp

    def _L0_tok_ref(x, W1, b1, W2, b2, W3, b3, W4, b4):
        import jax, jax.numpy as jnp
        import numpy as np
        T = 8
        a = jnp.einsum('bdl,od->blo', x, W1) + b1
        bs, L, d = a.shape
        zcol = jnp.zeros((bs, 1, d), a.dtype)
        shift_r = lambda v: jnp.concatenate([zcol, v[:, :-1]], axis=1)
        shift_l = lambda v: jnp.concatenate([v[:, 1:], zcol], axis=1)
        up = jnp.zeros_like(a)
        down = jnp.zeros_like(a)
        for _ in range(T):
            up = jax.nn.relu(a + shift_r(up) @ W2.T + b2)
            down = jax.nn.relu(a + shift_l(down) @ W2.T + b2)
        c = jnp.einsum('bdl,od->blo', x, W3) + b3
        miu = jax.nn.relu(c + (shift_r(up) @ W4.T + b4) + (shift_l(down) @ W4.T + b4))
        return miu

    def _L0_attn_ref(x, e, p, ln_scale, W_q, W_k, W_v, W_o, gamma):
        import jax, jax.numpy as jnp
        import numpy as np
        EPS = 1e-05

        def _ln(x, scale):
            mu = jnp.mean(x, axis=-1, keepdims=True)
            var = jnp.var(x, axis=-1, keepdims=True)
            return (x - mu) / jnp.sqrt(var + EPS) * scale
        B, S, E = x.shape
        H = W_q.shape[0]
        xn = _ln(x, ln_scale)
        Q = jnp.einsum('bse,hef->bhsf', xn, W_q)
        K = jnp.einsum('bse,hef->bhsf', xn, W_k)
        V = jnp.einsum('bse,hef->bhsf', xn, W_v)
        q2 = jnp.sum(Q * Q, axis=-1)[..., :, None]
        k2 = jnp.sum(K * K, axis=-1)[..., None, :]
        qk = jnp.einsum('bhsf,bhtf->bhst', Q, K)
        sqdist = jnp.maximum(q2 + k2 - 2.0 * qk, 0.0)
        scores = jnp.exp(-gamma * sqdist)
        out = jnp.einsum('bhst,bhtf->bhsf', scores, V)
        out = out.transpose(0, 2, 1, 3).reshape(B, S, H * E)
        return out @ W_o.T

    def _L0_ffn_ref(x, gate_w, gate_b, w1, b1, w2, b2, gamma, beta):
        import jax, jax.numpy as jnp
        import numpy as np
        B, S, H, F, E, K = (8, 1024, 64, 128, 16, 2)
        EPS = 1e-05
        gate_logits = x @ gate_w + gate_b
        topk_vals, topk_idx = jax.lax.top_k(gate_logits, K)
        topk_w = jax.nn.softmax(topk_vals, axis=-1)
        h = jax.nn.relu(jnp.einsum('bsh,ehf->bsef', x, w1) + b1)
        expert_out = jnp.einsum('bsef,efh->bseh', h, w2) + b2
        sel = jnp.take_along_axis(expert_out, topk_idx[:, :, :, None], axis=2)
        moe = jnp.sum(topk_w[..., None] * sel, axis=2)
        y = x + moe
        mu = jnp.mean(y, axis=-1, keepdims=True)
        var = jnp.var(y, axis=-1, keepdims=True)
        return (y - mu) / jnp.sqrt(var + EPS) * gamma + beta
    h = _L0_tok_ref(x, L0_tok_W1, L0_tok_b1, L0_tok_W2, L0_tok_b2, L0_tok_W3, L0_tok_b3, L0_tok_W4, L0_tok_b4)
    h = h + _L0_attn_ref(_layernorm(h, axis=-1), L0_attn_e, L0_attn_p, L0_attn_ln_scale, L0_attn_W_q, L0_attn_W_k, L0_attn_W_v, L0_attn_W_o, L0_attn_gamma)
    h = h + _L0_ffn_ref(_layernorm(h, axis=-1), L0_ffn_gate_w, L0_ffn_gate_b, L0_ffn_w1, L0_ffn_b1, L0_ffn_w2, L0_ffn_b2, L0_ffn_gamma, L0_ffn_beta)
    return h

_drawn_inputs = setup_inputs


def setup_inputs(seed=0):
    import zlib

    import numpy as np

    out = dict(_drawn_inputs(seed))
    spreads = {'L0_attn_ln_scale': (1.0, 0.2),
     'L0_attn_gamma': (1.0, 0.2),
     'L0_ffn_gate_b': (0.0, 0.1),
     'L0_ffn_b1': (0.0, 0.8),
     'L0_ffn_b2': (0.0, 0.1),
     'L0_ffn_gamma': (1.0, 0.2),
     'L0_ffn_beta': (0.0, 0.1)}
    factors = {'L0_ffn_w1': 5.306, 'L0_ffn_w2': 3.525}
    for name, (base, spread) in spreads.items():
        noise = np.random.default_rng([zlib.crc32(name.encode()), seed]).standard_normal(out[name].shape)
        drawn = base * np.exp(spread * noise) if base else spread * noise
        out[name] = jnp.asarray(drawn.astype(out[name].dtype))
    for name, factor in factors.items():
        out[name] = (out[name] * factor).astype(out[name].dtype)
    return out
```

```python
from contextlib import ExitStack

import numpy as np

import concourse.bass as bass
from concourse import mybir

ALU = mybir.AluOpType
ACT = mybir.ActivationFunctionType
AX = mybir.AxisListType
F32 = mybir.dt.float32
F32R = mybir.dt.float32r
ds = bass.ds

B, D_IN, L = 32, 4, 250
D = 64
H = 8
E = 16
F = 128
STEPS = 8
T = L // 2
PAIRS = B // 2
C = 2 * L
CH = 4
NCHUNK = PAIRS * CH
CHAINS = 4
EPS = 1e-5
BIG = 3.0e38

XROWS = 4 * D_IN
AROWS = 2 * XROWS + 2
Q_ROW, ONE_ROW, K_ROW, S_ROWS = 64, 80, 96, 112

W_ROWS = 96

C_IDENT, C_FOLD = 0, 128
C_MX, C_MW, C_MS1, C_MS2, C_MG = 192, 193, 194, 195, 196
C_IND, C_SEL = 197, 205
C_COLS = 221


def constants():
    c = np.zeros((128, C_COLS), np.float32)
    c[:, C_IDENT:C_IDENT + 128] = np.eye(128)
    c[:64, C_FOLD:C_FOLD + 64] = np.eye(64)
    c[64:, C_FOLD:C_FOLD + 64] = np.eye(64)
    for half in range(2):
        for g in range(4):
            rows = slice(half * XROWS + g * D_IN, half * XROWS + (g + 1) * D_IN)
            c[rows, C_MX] = -1.0 if g >= 2 else 0.0
            c[rows, C_MW] = -1.0 if g % 2 else 0.0
    c[AROWS - 1, C_MW] = -1.0
    c[64:, C_MS1] = -1.0
    c[Q_ROW + H:Q_ROW + 2 * H, C_MS2] = -1.0
    c[K_ROW + H:K_ROW + 2 * H, C_MS2] = -1.0
    c[32:32 + E, C_MG] = -1.0
    for h in range(H):
        c[K_ROW + h, C_IND + h] = 1.0
        c[K_ROW + H + h, C_IND + h] = 1.0
    for e in range(E):
        c[e, C_SEL + e] = 1.0
        c[32 + e, C_SEL + e] = 1.0
    return c


def build(nc, cst, xr, aw1, aw2, cw1, cw2, w2bd, w4dup, wqT, wkT, wvT, woT, wq, wk, gam, lns,
          gw, gb, w1, b1, w2, b2, fg, fb, out):
    with ExitStack() as ctx:
        def sb(name, shape, dt=F32):
            return ctx.enter_context(nc.sbuf_tensor(name, shape, dt))

        def sem(name):
            return ctx.enter_context(nc.semaphore(name))

        def f32(ap):
            return ap.bitcast(F32)

        bank = [ctx.enter_context(nc.psum_tensor(f"bank{i}", [128, 512], F32)) for i in range(8)]

        c_sb = sb("c_sb", [128, C_COLS])
        ident = c_sb[:, C_IDENT:C_IDENT + 128]
        fold = c_sb[:, C_FOLD:C_FOLD + 64]
        aw1_sb, aw2_sb = sb("aw1_sb", [AROWS, 128]), sb("aw2_sb", [AROWS, 128])
        cw1_sb, cw2_sb = sb("cw1_sb", [AROWS, 128]), sb("cw2_sb", [AROWS, 128])
        w2bd_sb, w4_sb = sb("w2bd_sb", [128, 128]), sb("w4_sb", [128, 128])
        gam_sb, lns_sb = sb("gam_sb", [128, H]), sb("lns_sb", [T, D])
        gwraw, gb_sb = sb("gwraw", [128, E]), sb("gb_sb", [T, E])
        b1_sb, w2_sb = sb("b1_sb", [F, E]), sb("w2_sb", [F, E, D])
        b2raw = sb("b2raw", [48, 128])
        fg_sb, fb_sb = sb("fg_sb", [T, D]), sb("fb_sb", [T, D])

        aw, cw = sb("aw", [AROWS, 128], F32R), sb("cw", [AROWS, 128], F32R)
        awt = sb("awt", [AROWS, 2, 128])
        awr = sb("awr", [AROWS, 2, 128], F32R)
        wqku_hi = sb("wqku_hi", [128, 3, H * D], F32R)
        wqku_lo = sb("wqku_lo", [128, 3, H * D], F32R)
        wg_hi, wg_lo = sb("wg_hi", [128, H, 2, D], F32R), sb("wg_lo", [128, H, 2, D], F32R)
        gw_hi, gw_lo = sb("gw_hi", [128, E], F32R), sb("gw_lo", [128, E], F32R)
        w1_hi, w1_lo = sb("w1_hi", [128, E, F], F32R), sb("w1_lo", [128, E, F], F32R)
        b2_hi, b2_lo = sb("b2_hi", [48, 128], F32R), sb("b2_lo", [48, 128], F32R)
        sel = sb("sel", [48, E, 128], F32R)
        g2 = sb("g2", [128, H])
        gneg = sb("gneg", [128, H])
        cap_lo, cap_hi = sb("cap_lo", [128, H]), sb("cap_hi", [128, H])
        spare, spare2 = sb("spare", [T, 1]), sb("spare2", [T, 1])
        mhalf, eps = sb("mhalf", [T, CH]), sb("eps", [T, CH])

        h_all = sb("h_all", [T, NCHUNK, D])

        stats, aggr = sb("stats", [T, CH, 6]), sb("aggr", [T, CH, 2])
        inv = sb("inv", [T, 8, CH])
        z = sb("z", [T, CH, D])
        xn = sb("xn", [T, CH, 2, D])
        rnd1, rnd2 = sb("rnd1", [128, C], F32R), sb("rnd2", [128, C], F32R)
        s1 = [sb(f"s1_{j}", [128, C], F32R) for j in range(2)]
        s2 = [sb(f"s2_{j}", [S_ROWS, C], F32R) for j in range(2)]
        m2 = [sb(f"m2_{j}", [S_ROWS, H, C], F32R) for j in range(2)]
        qk = sb("qk", [T, CH, 2, H])
        qkw = sb("qkw", [T, CH, S_ROWS])

        lg = sb("lg", [T, 8, CH, E])
        top = sb("top", [T, 12, CH])
        desc = sb("desc", [T, E])
        wtok = sb("wtok", [T, CH, W_ROWS])
        wt = [sb(f"wt{j}", [48, C], F32R) for j in range(2)]

        def phase(*tensors):
            with ExitStack() as scope:
                return [[scope.enter_context(nc.sbuf_tensor(f"{name}{j}", shape, dt)) for j in range(n)]
                        for name, n, shape, dt in tensors]

        x_raw, x_rnd, x_st, state, shifted, miu, (wqT_sb,), (wkT_sb,), (wvT_sb,), (woT_sb,), (wraw,), (w1raw,) = phase(
            ("x_raw", CHAINS, [2 * XROWS, C], F32), ("x_rnd", CHAINS, [2 * XROWS, C], F32R),
            ("x_st", CHAINS, [AROWS, C], F32R), ("state", CHAINS, [128, 2, L + 1], F32),
            ("shifted", CHAINS, [128, 2, L], F32), ("miu", CHAINS, [128, C], F32),
            ("wqT_sb", 1, [64, H, 128], F32), ("wkT_sb", 1, [64, H, 64], F32),
            ("wvT_sb", 1, [64, H, 128], F32), ("woT_sb", 1, [64, H, 64], F32),
            ("wraw", 1, [128, 4, H * D], F32), ("w1raw", 1, [128, E, F], F32))
        m1, u_sb, sq, prob, (y_att,) = phase(
            ("m1_", 2, [128, H, C], F32R), ("u", 2, [T, CH, H * D], F32), ("sq", 2, [T, H * D], F32),
            ("prob", 4, [T, 2, L], F32), ("y_att", 1, [128, L], F32))
        relu_sb, gated, (y_moe,), (yt,), (stats2,), (aggr2,), (inv2,), (yz,), (res,), (hn_all,) = phase(
            ("relu", 2, [F, C], F32), ("gated", 4, [F, C], F32), ("y_moe", 1, [128, C], F32),
            ("yt", 1, [T, CH, D], F32), ("stats2_", 1, [T, CH, 6], F32), ("aggr2_", 1, [T, CH, 2], F32),
            ("inv2_", 1, [T, 4, CH], F32), ("yz", 1, [T, 3, CH, D], F32), ("res", 1, [T, CH, D], F32),
            ("hn_all", 1, [T, NCHUNK, D], F32))

        ld_a, ld_b, ld_c = sem("ld_a"), sem("ld_b"), sem("ld_c")
        s_prep = sem("s_prep")
        s_prepg = sem("s_prepg")
        s_wprod = sem("s_wprod")
        a_xin = [sem(f"a_xin{j}") for j in range(CHAINS)]
        a_rnd, a_x = sem("a_rnd"), sem("a_x")
        a_mm = [sem(f"a_mm{j}") for j in range(CHAINS)]
        a_st = [sem(f"a_st{j}") for j in range(CHAINS)]
        a_c, a_miu0, a_miu1, a_t, a_h = (sem(n) for n in ("a_c", "a_miu0", "a_miu1", "a_t", "a_h"))
        b_ln, b_inv, b_z, b_xn = (sem(n) for n in ("b_ln", "b_inv", "b_z", "b_xn"))
        b_xt, b_rnd, b_s1 = sem("b_xt"), sem("b_rnd"), sem("b_s1")
        b_pj, b_ev, b_red, b_gl = sem("b_pj"), sem("b_ev"), sem("b_red"), sem("b_gl")
        b_qkw, b_qt, b_rnd2, b_s2, b_row = (sem(n) for n in ("b_qkw", "b_qt", "b_rnd2", "b_s2", "b_row"))
        b_sc, b_exp, b_cap, b_pv = sem("b_sc"), sem("b_exp"), sem("b_cap"), sem("b_pv")
        b_y, b_f, b_res = sem("b_y"), sem("b_f"), sem("b_res")
        c_ln, c_inv, c_hn, c_xn = (sem(n) for n in ("c_ln", "c_inv", "c_hn", "c_xn"))
        c_xt, c_rnd, c_s1, c_lg = (sem(n) for n in ("c_xt", "c_rnd", "c_s1", "c_lg"))
        c_gate, c_e, c_wtt, c_rndw, c_wt = (sem(n) for n in ("c_gate", "c_e", "c_wtt", "c_rndw", "c_wt"))
        c_up, c_wb, c_relu, c_gated, c_dn = (sem(n) for n in ("c_up", "c_wb", "c_relu", "c_gated", "c_dn"))
        c_y, c_f, c_fin, c_pinv, c_gres, c_pout, c_out = (
            sem(n) for n in ("c_y", "c_f", "c_fin", "c_pinv", "c_gres", "c_pout", "c_out"))

        def wait(eng, s, value):
            if not (isinstance(value, int) and value <= 0):
                eng.wait_ge(s, value)

        A_LOADS = [(c_sb, cst), (aw1_sb, aw1), (aw2_sb, aw2), (cw1_sb, cw1), (cw2_sb, cw2),
                   (w2bd_sb, w2bd), (w4_sb, w4dup), (gam_sb, gam), (wqT_sb, wqT), (wkT_sb, wkT),
                   (wvT_sb, wvT), (woT_sb, woT)]
        B_LOADS = [(wraw[:, 0, :], wq), (wraw[:, 1, :], wk), (lns_sb, lns), (gwraw, gw), (gb_sb, gb),
                   (w1raw, w1), (b1_sb, b1), (w2_sb, w2), (b2raw, b2), (fg_sb, fg), (fb_sb, fb)]

        BODY_B = (3, PAIRS - 1)
        BODY_C = (3, PAIRS - 1)

        def steps(eng, step, body):
            first, last = body
            for p in range(first):
                step(p, p % 2, p >= 2, p >= 1, True, True)
            with eng.Fori(0, (last - first) // 2) as i:
                for k in range(2):
                    step(i * 2 + (first + k), (first + k) % 2, True, True, True, True)
            for p in range(last, PAIRS + 2):
                step(p, p % 2, p - 2 < PAIRS, p - 1 < PAIRS, p < PAIRS, p + 1 < PAIRS)

        block = ctx.enter_context(nc.Block())

        @block.sync
        def _(sp):
            def full(t):
                return t[tuple(slice(None) for _ in t.shape)]

            for dst, src in A_LOADS:
                sp.dma_start(full(dst), full(src)).then_inc(ld_a, 16)
            for j in range(CHAINS):
                sp.dma_start(x_raw[j][:, :], xr[j, :, :]).then_inc(a_xin[j], 16)
            for dst, src in B_LOADS:
                sp.dma_start(full(dst), full(src)).then_inc(ld_b, 16)

            with sp.Fori(1, PAIRS // CHAINS) as i:
                for j in range(CHAINS):
                    sp.wait_ge(a_x, i * CHAINS - (CHAINS - 1 - j))
                    sp.dma_start(x_raw[j][:, :], xr[ds(i * CHAINS + j, 1), :, :].rearrange("a r c -> (a r) c"))\
                        .then_inc(a_xin[j], 16)

            def step_b(p, j, old2, old, new, ln):
                if new:
                    sp.wait_ge(b_s2, p + 1)
                    wait(sp, b_sc, 16 * (p - 1))
                    for k in range(2):
                        sp.dma_start(f32(m2[j][ONE_ROW + k:ONE_ROW + k + 1, :, :]),
                                     f32(s2[j][Q_ROW + k * H:Q_ROW + (k + 1) * H, :])).then_inc(b_row, 16)

            steps(sp, step_b, BODY_B)

            with sp.Fori(0, PAIRS) as i:
                sp.wait_ge(c_pout, i + 1)
                sp.dma_start(out[ds(i * 2, 2), :, :].rearrange("b (k t) d -> t (b k) d", k=2), res[:, :, :])\
                    .then_inc(c_out, 16)
            sp.wait_ge(c_out, 16 * PAIRS)

        @block.gpsimd
        def _(gp):
            count = [0]

            def done(ins):
                count[0] += 1
                ins.then_inc(s_prepg, 1)
                gp.wait_ge(s_prepg, count[0])

            for j in range(CHAINS):
                done(gp.memset(state[j][:, :, :], 0.0))
                done(gp.memset(shifted[j][:, :, :], 0.0))
                done(gp.memset(f32(x_st[j][32:34, :]), 1.0))
            for j in range(2):
                done(gp.memset(f32(m2[j][64:96, :, :]), 0.0))
            done(gp.memset(qkw[:, :, :], 0.0))
            done(gp.memset(wtok[:, :, :], 0.0))
            for counter in (a_c, a_h):
                gp.memset(spare2[:, :], 0.0).then_inc(counter, 1)
                gp.wait_ge(counter, 1)
            done(gp.memset(eps[:, :], EPS))
            done(gp.memset(mhalf[:, :], -0.5))
            done(gp.memset(qkw[:, :, ONE_ROW:ONE_ROW + 2], 1.0))
            done(gp.iota(lg[:, 7, 0, :].bitcast(mybir.dt.int32), [[-1, E]], base=E, channel_multiplier=0))
            done(gp.tensor_copy(desc[:, :], lg[:, 7, 0, :].bitcast(mybir.dt.int32)))

            gp.wait_ge(ld_a, 16 * len(A_LOADS))
            gp.wait_ge(ld_b, 16 * len(B_LOADS))
            for j in range(2):
                done(gp.tensor_copy(m2[j][K_ROW:S_ROWS, :, :],
                                    c_sb[K_ROW:S_ROWS, C_IND:C_IND + H].unsqueeze(2).to_broadcast([2 * H, H, C])))
            for rows in (slice(0, 32), slice(32, 48)):
                n = rows.stop - rows.start
                done(gp.tensor_copy(sel[rows, :, :], c_sb[rows, C_SEL:C_SEL + E].unsqueeze(2).to_broadcast([n, E, 128])))
            gp.wait_ge(s_prep, PREP_W)
            for q, src in ((0, 0), (1, 1), (2, 3)):
                done(gp.tensor_copy(wqku_hi[:, q, :], wraw[:, src, :]))
            graw = wraw[:, 2, :].rearrange("p (h d) -> p h d", h=H)
            for k in range(2):
                done(gp.tensor_copy(wg_hi[:, :, k, :], graw))
            done(gp.tensor_copy(gw_hi[:, :], gwraw[:, :]))
            done(gp.tensor_copy(b2_hi[:, :], b2raw[:, :]))
            done(gp.tensor_copy(w1_hi[:, :, :], w1raw[:, :, :]))
            for q, src in ((0, 0), (1, 1), (2, 3)):
                done(gp.tensor_tensor(wqku_lo[:, q, :], wraw[:, src, :], f32(wqku_hi[:, q, :]), ALU.subtract))
            for k in range(2):
                done(gp.tensor_tensor(wg_lo[:, :, k, :], graw, f32(wg_hi[:, :, k, :]), ALU.subtract))
            done(gp.tensor_tensor(gw_lo[:, :], gwraw[:, :], f32(gw_hi[:, :]), ALU.subtract))
            done(gp.tensor_tensor(b2_lo[:, :], b2raw[:, :], f32(b2_hi[:, :]), ALU.subtract))
            done(gp.tensor_tensor(w1_lo[:, :, :], w1raw[:, :, :], f32(w1_hi[:, :, :]), ALU.subtract))
            assert count[0] == PREP_G

            lns4 = lns_sb[:, :].unsqueeze(1).unsqueeze(1).to_broadcast([T, CH, 2, D])
            gneg4 = gneg[0:T, :].unsqueeze(1).unsqueeze(1).to_broadcast([T, CH, 2, H])

            def b_scales(p):
                n = 7 * p
                gp.wait_ge(b_ln, 2 * p + 2)
                wait(gp, b_z, p)
                var = aggr[:, :, 1]
                gp.tensor_tensor(inv[:, 0, :], var, eps[:, :], ALU.add).then_inc(b_inv, 1)
                gp.wait_ge(b_inv, n + 1)
                gp.tensor_tensor(inv[:, 1, :], inv[:, 0, :], mhalf[:, :], ALU.pow).then_inc(b_inv, 1)
                gp.wait_ge(b_inv, n + 2)
                gp.tensor_tensor(inv[:, 2, :], var, inv[:, 1, :], ALU.mult).then_inc(b_inv, 1)
                gp.wait_ge(b_inv, n + 3)
                gp.tensor_tensor(inv[:, 3, :], inv[:, 2, :], inv[:, 1, :], ALU.mult).then_inc(b_inv, 1)
                gp.wait_ge(b_inv, n + 4)
                gp.tensor_tensor(inv[:, 4, :], inv[:, 3, :], eps[:, :], ALU.add).then_inc(b_inv, 1)
                gp.wait_ge(b_inv, n + 5)
                gp.tensor_tensor(inv[:, 5, :], inv[:, 4, :], mhalf[:, :], ALU.pow).then_inc(b_inv, 1)
                gp.wait_ge(b_inv, n + 6)
                gp.tensor_tensor(inv[:, 6, :], inv[:, 1, :], inv[:, 5, :], ALU.mult).then_inc(b_inv, 1)
                gp.wait_ge(b_z, p + 1)
                wait(gp, b_xt, p)
                gp.tensor_tensor(xn[:, :, :, :], z[:, :, :].unsqueeze(2).to_broadcast([T, CH, 2, D]),
                                 lns4, ALU.mult).then_inc(b_xn, 1)

            def step_b(p, j, old2, old, new, ln):
                if isinstance(p, int) and p == 0:
                    b_scales(0)
                if new:
                    gp.wait_ge(b_red, 8 * p + 8)
                    wait(gp, b_qt, p)
                    gp.tensor_tensor(
                        qkw[:, :, Q_ROW:Q_ROW + 2 * H].rearrange("p c (a h) -> p c a h", a=2),
                        qk[:, :, 0, :].unsqueeze(2).to_broadcast([T, CH, 2, H]), gneg4, ALU.mult).then_inc(b_qkw, 1)
                    gp.tensor_tensor(
                        qkw[:, :, K_ROW:K_ROW + 2 * H].rearrange("p c (a h) -> p c a h", a=2),
                        qk[:, :, 1, :].unsqueeze(2).to_broadcast([T, CH, 2, H]), gneg4, ALU.mult).then_inc(b_qkw, 1)
                if ln:
                    b_scales(p + 1)

            steps(gp, step_b, BODY_B)

            def c_scales(p):
                gp.wait_ge(c_ln, 2 * p + 2)
                wait(gp, c_hn, p)
                gp.tensor_tensor(inv[:, 0, :], aggr[:, :, 1], eps[:, :], ALU.add).then_inc(c_inv, 1)
                gp.wait_ge(c_inv, 2 * p + 1)
                gp.tensor_tensor(inv[:, 1, :], inv[:, 0, :], mhalf[:, :], ALU.pow).then_inc(c_inv, 1)
                gp.wait_ge(c_hn, p + 1)
                wait(gp, c_xt, p)
                gp.tensor_copy(xn[:, :, :, :], hn_all[:, ds(p * CH, CH), :].unsqueeze(2).to_broadcast([T, CH, 2, D]))\
                    .then_inc(c_xn, 1)

            def c_result(p):
                gp.wait_ge(c_fin, 4 * p + 3)
                gp.tensor_tensor(inv2[:, 0, :], aggr2[:, :, 1], eps[:, :], ALU.add).then_inc(c_pinv, 1)
                gp.wait_ge(c_pinv, 2 * p + 1)
                gp.tensor_tensor(inv2[:, 1, :], inv2[:, 0, :], mhalf[:, :], ALU.pow).then_inc(c_pinv, 1)
                gp.wait_ge(c_fin, 4 * p + 4)
                gp.tensor_tensor(yz[:, 1, :, :], yz[:, 0, :, :], fg_sb[:, :].unsqueeze(1).to_broadcast([T, CH, D]),
                                 ALU.mult).then_inc(c_gres, 1)
                gp.wait_ge(c_gres, 2 * p + 1)
                gp.tensor_tensor(yz[:, 2, :, :], yz[:, 1, :, :], fb_sb[:, :].unsqueeze(1).to_broadcast([T, CH, D]),
                                 ALU.add).then_inc(c_gres, 1)
                gp.wait_ge(c_gres, 2 * p + 2)
                wait(gp, c_out, 16 * p)
                gp.tensor_tensor(res[:, :, :], yz[:, 2, :, :], h_all[:, ds(p * CH, CH), :], ALU.add).then_inc(c_pout, 1)

            def step_c(p, j, old2, old, new, ln):
                if isinstance(p, int) and p == 0:
                    c_scales(0)
                if old2:
                    c_result(p - 2)
                if ln:
                    c_scales(p + 1)

            steps(gp, step_c, BODY_C)

        @block.scalar
        def _(act):
            def evac(j, k, i):
                act.wait_ge(a_mm[j], i * STEPS + k + 1)
                ps = bank[j][:, 0:C].rearrange("p (b l) -> p b l", b=2)
                if k < STEPS - 1:
                    act.activation(state[j][:, :, 1:L + 1], ps, ACT.Relu).then_inc(a_st[j], 2)
                else:
                    act.wait_ge(a_c, i * CHAINS + 1)
                    act.activation(shifted[j][0:64, :, 1:L], ps[0:64, :, 0:L - 1], ACT.Relu).then_inc(a_st[j], 1)
                    act.activation(shifted[j][64:128, :, 0:L - 1], ps[64:128, :, L - 2::-1], ACT.Relu)\
                        .then_inc(a_st[j], 1)

            with act.Fori(0, PAIRS // CHAINS) as i:
                for j in range(CHAINS):
                    act.wait_ge(a_xin[j], i * 16 + 16)
                    act.activation(x_rnd[j][:, :], x_raw[j][:, :], ACT.Copy).then_inc(a_rnd, 1)
                for k in range(STEPS):
                    for j in range(0, CHAINS, 2):
                        evac(j, k, i)
                for j in range(0, CHAINS, 2):
                    act.wait_ge(a_c, i * CHAINS + j + 2)
                    act.activation(miu[j][:, :], bank[4 + j][:, 0:C], ACT.Relu).then_inc(a_miu0, 1)
                for j in range(0, CHAINS, 2):
                    act.wait_ge(a_t, i * CHAINS + j + 1)
                    act.activation(h_all[:, ds(i * CHAINS * CH + j * CH, CH), :],
                                   bank[j][0:T, :].rearrange("p (c d) -> p c d", c=CH)[:, :, 0:D], ACT.Copy)\
                        .then_inc(a_h, 1)

            def evac_y(p, b):
                act.wait_ge(b_pv, 8 * p + 4 * b + 4)
                wait(act, b_f, 2 * p + b)
                act.activation(y_att[:, :], bank[1][:, 0:L], ACT.Copy).then_inc(b_y, 1)

            def step_b(p, j, old2, old, new, ln):
                for v in range(8):
                    if old:
                        for c in range(2):
                            n = 2 * v + c
                            act.wait_ge(b_sc, 16 * (p - 1) + n + 1)
                            wait(act, b_pv, 8 * (p - 1) + v - 1)
                            act.activation(prob[n % 4][:, :, :],
                                           bank[4 + n % 4][0:T, 0:C].rearrange("p (h l) -> p h l", h=2),
                                           ACT.Exp).then_inc(b_exp, 1)
                    if v == 0 and old2:
                        evac_y(p - 2, 1)
                    if v == 4 and old:
                        evac_y(p - 1, 0)
                    if new and v == 0:
                        act.wait_ge(b_xt, p + 1)
                        wait(act, b_s1, p)
                        act.activation(rnd1[:, :], bank[0][:, 0:C], ACT.Copy).then_inc(b_rnd, 1)
                        wait(act, b_sc, 16 * (p - 1))
                        act.activation(s2[j][0:64, :], bank[0][0:64, 0:C], ACT.Copy).then_inc(b_rnd, 1)
                    if new and 1 <= v <= 4:
                        c = v - 1
                        for q in range(2):
                            act.wait_ge(b_pj, 20 * p + 3 * c + q + 1)
                            wait(act, b_red, 8 * p + 2 * c + q - 1)
                            act.activation(sq[q][:, :], bank[2 + (3 * c + q) % 2][0:T, :], ACT.Square)\
                                .then_inc(b_ev, 1)
                        act.wait_ge(b_pj, 20 * p + 3 * c + 3)
                        wait(act, b_pv, 8 * (p - 1))
                        act.activation(u_sb[j][:, c, :], bank[2 + (3 * c + 2) % 2][0:T, :], ACT.Copy)\
                            .then_inc(b_ev, 1)
                    if new and v >= 5:
                        for h in range(3 * (v - 5), min(3 * (v - 5) + 3, H)):
                            act.wait_ge(b_pj, 20 * p + 12 + h + 1)
                            wait(act, b_sc, 16 * (p - 1))
                            act.activation(m1[j][:, h, :], bank[2 + h % 2][:, 0:C], ACT.Copy).then_inc(b_ev, 1)
                    if new and v == 6:
                        act.wait_ge(b_qt, p + 1)
                        wait(act, b_s2, p)
                        act.activation(rnd2[64:S_ROWS, :], bank[0][64:S_ROWS, 0:C], ACT.Copy).then_inc(b_rnd2, 1)

            def step_b_tail(p, j, old2, old, new, ln):
                if isinstance(p, int) and p == PAIRS + 1:
                    evac_y(p - 2, 1)
                else:
                    step_b(p, j, old2, old, new, ln)

            steps(act, step_b_tail, BODY_B)

            def step_c(p, j, old2, old, new, ln):
                for v in range(8):
                    if old:
                        for e in (2 * v, 2 * v + 1):
                            act.wait_ge(c_up, 16 * (p - 1) + e + 1)
                            wait(act, c_gated, 16 * (p - 1) + e - 1)
                            act.activation(relu_sb[e % 2][:, :], bank[2 + e % 2][:, 0:C], ACT.Relu,
                                           bias=b1_sb[:, e:e + 1]).then_inc(c_relu, 1)
                    if old2 and v == 0:
                        act.wait_ge(c_dn, 8 * (p - 2) + 8)
                        wait(act, c_f, p - 2)
                        act.activation(y_moe[:, :], bank[6 + (j % 2)][:, 0:C], ACT.Copy).then_inc(c_y, 1)
                    if new and v == 0:
                        act.wait_ge(c_xt, p + 1)
                        wait(act, c_s1, p)
                        act.activation(rnd1[:, :], bank[0][:, 0:C], ACT.Copy).then_inc(c_rnd, 1)
                    if new and v == 3:
                        act.wait_ge(c_gate, GATE * p + GATE_D)
                        act.activation(top[:, 7, :], top[:, 6, :], ACT.Exp).then_inc(c_e, 1)
                    if new and v == 5:
                        act.wait_ge(c_wtt, p + 1)
                        wait(act, c_wt, p)
                        act.activation(rnd2[0:48, :], bank[0][0:48, 0:C], ACT.Copy).then_inc(c_rndw, 1)

            steps(act, step_c, BODY_C)

        @block.vector
        def _(dve):
            count = [0]

            def done(ins):
                count[0] += 1
                ins.then_inc(s_prep, 1)
                dve.wait_ge(s_prep, count[0])

            dve.wait_ge(ld_a, 16 * len(A_LOADS))
            done(dve.tensor_tensor(awt[:, 0, :], aw1_sb[:, :], aw2_sb[:, :], ALU.add))
            done(dve.scalar_tensor_tensor(awt[:, 1, :], cw2_sb[:, :], 2.0, cw1_sb[:, :], ALU.mult, ALU.add))
            done(dve.tensor_copy(awr[:, :, :], awt[:, :, :]))
            mw = c_sb[0:AROWS, C_MW:C_MW + 1]
            dve.scalar_tensor_tensor(aw[:, :], f32(awr[:, 0, :]), mw, awt[:, 0, :], ALU.mult, ALU.add)
            done(dve.scalar_tensor_tensor(cw[:, :], f32(awr[:, 1, :]), mw, awt[:, 1, :], ALU.mult, ALU.add))
            assert count[0] == PREP_A
            dve.tensor_scalar(g2[:, :], gam_sb[:, :], 2.0, None, ALU.mult)
            dve.tensor_scalar(gneg[:, :], gam_sb[:, :], -1.0, None, ALU.mult)
            done(dve.tensor_scalar(cap_lo[:, :], gam_sb[:, :], 0.0, None, ALU.is_lt))
            done(dve.tensor_scalar(cap_hi[:, :], cap_lo[:, :], BIG, 1.0, ALU.mult, ALU.add))
            dve.wait_ge(s_wprod, 1)
            dve.tensor_tensor(wraw[:, 2, :].rearrange("p (h d) -> p h d", h=H),
                              bank[6][:, :].rearrange("p (h d) -> p h d", h=H),
                              g2[:, :].unsqueeze(2).to_broadcast([128, H, D]), ALU.mult)
            done(dve.tensor_copy(wraw[:, 3, :], bank[7][:, :]))
            assert count[0] == PREP_W

            def evac(j, k, i):
                dve.wait_ge(a_mm[j], i * STEPS + k + 1)
                ps = bank[j][:, 0:C].rearrange("p (b l) -> p b l", b=2)
                if k < STEPS - 1:
                    dve.tensor_scalar(state[j][:, :, 1:L + 1], ps, 0.0, None, ALU.max).then_inc(a_st[j], 2)
                else:
                    dve.wait_ge(a_c, i * CHAINS + 1)
                    dve.tensor_scalar(shifted[j][0:64, :, 1:L], ps[0:64, :, 0:L - 1], 0.0, None, ALU.max)\
                        .then_inc(a_st[j], 1)
                    dve.tensor_scalar(shifted[j][64:128, :, 0:L - 1], ps[64:128, :, L - 2::-1], 0.0, None, ALU.max)\
                        .then_inc(a_st[j], 1)

            dve.wait_ge(s_prepg, PREP_GA)
            with dve.Fori(0, PAIRS // CHAINS) as i:
                for j in range(CHAINS):
                    dve.wait_ge(a_rnd, i * CHAINS + j + 1)
                    if j == 0:
                        dve.wait_ge(a_c, i * CHAINS + 1)
                    dve.scalar_tensor_tensor(x_st[j][0:2 * XROWS, :], f32(x_rnd[j][:, :]),
                                             c_sb[0:2 * XROWS, C_MX:C_MX + 1], x_raw[j][:, :],
                                             ALU.mult, ALU.add).then_inc(a_x, 1)
                for k in range(STEPS):
                    for j in range(1, CHAINS, 2):
                        evac(j, k, i)
                for j in range(1, CHAINS, 2):
                    dve.wait_ge(a_c, i * CHAINS + j + 2)
                    dve.tensor_scalar(miu[j][:, :], bank[4 + j][:, 0:C], 0.0, None, ALU.max).then_inc(a_miu1, 1)
                for j in range(1, CHAINS, 2):
                    dve.wait_ge(a_t, i * CHAINS + j + 1)
                    dve.tensor_copy(h_all[:, ds(i * CHAINS * CH + j * CH, CH), :],
                                    bank[j][0:T, :].rearrange("p (c d) -> p c d", c=CH)[:, :, 0:D]).then_inc(a_h, 1)

            def norm(p, s_ln, s_inv, invs, row, s_out, dst, at):
                for c in range(CH):
                    last = dve.bn_stats(stats[:, c, :], h_all[:, ds(p * CH + c, 1), :])
                last.then_inc(s_ln, 1)
                dve.wait_ge(s_ln, 2 * p + 1)
                dve.memset(spare[:, :], 0.0)
                for c in range(CH):
                    last = dve.bn_aggr(aggr[:, c, :], stats[:, c, :])
                last.then_inc(s_ln, 1)
                dve.wait_ge(s_ln, 2 * p + 2)
                dve.wait_ge(s_inv, invs * (p + 1))
                for c in range(CH):
                    last = dve.tensor_scalar(dst[:, at(c), :], h_all[:, ds(p * CH + c, 1), :],
                                             aggr[:, c, 0:1], inv[:, row, c:c + 1], ALU.subtract, ALU.mult)
                last.then_inc(s_out, 1)

            def norm_b(p):
                wait(dve, b_xn, p)
                norm(p, b_ln, b_inv, 7, 6, b_z, z, lambda c: slice(c, c + 1))

            def residual(p, b):
                dve.wait_ge(b_f, 2 * p + b + 1)
                rows = h_all[:, ds(p * CH + 2 * b, 2), :]
                dve.tensor_tensor(rows, bank[0][0:T, 0:2 * D].rearrange("p (c d) -> p c d", c=2), rows, ALU.add)\
                    .then_inc(b_res, 1)

            def step_b(p, j, old2, old, new, ln):
                if isinstance(p, int) and p == 0:
                    dve.wait_ge(a_h, PAIRS + 1)
                    norm_b(0)
                for v in range(8):
                    if old:
                        for c in range(2):
                            n = 2 * v + c
                            dve.wait_ge(b_exp, 16 * (p - 1) + n + 1)
                            for hh in range(2):
                                h = (2 * v + hh) % H
                                part = prob[n % 4][:, hh, :]
                                last = dve.tensor_scalar(part, part, cap_hi[0:T, h:h + 1], cap_lo[0:T, h:h + 1],
                                                         ALU.min, ALU.max)
                            last.then_inc(b_cap, 1)
                    if v == 1 and old2:
                        residual(p - 2, 1)
                    if v == 6 and old:
                        residual(p - 1, 0)
                    if new and v == 0:
                        dve.wait_ge(b_rnd, 2 * p + 2)
                        wait(dve, b_sc, 16 * (p - 1))
                        dve.scalar_tensor_tensor(s1[j][:, :], f32(rnd1[:, :]), c_sb[:, C_MS1:C_MS1 + 1],
                                                 bank[0][:, 0:C], ALU.mult, ALU.add).then_inc(b_s1, 1)
                    if new and 1 <= v <= 4:
                        c = v - 1
                        if c == 0:
                            wait(dve, b_qkw, 2 * p)
                        for q in range(2):
                            dve.wait_ge(b_ev, 20 * p + 3 * c + q + 1)
                            dve.tensor_reduce(qk[:, c, q, :], sq[q][:, :].rearrange("p (h d) -> p h d", h=H),
                                              AX.X, ALU.add).then_inc(b_red, 1)
                    if new and v >= 5:
                        for h in range(3 * (v - 5), min(3 * (v - 5) + 3, H)):
                            dve.wait_ge(b_ev, 20 * p + 12 + h + 1)
                            dve.tensor_tensor(m2[j][0:64, h, :], bank[2 + h % 2][0:64, 0:C], f32(m1[j][0:64, h, :]),
                                              ALU.subtract).then_inc(b_gl, 1)
                    if new and v == 6:
                        dve.wait_ge(b_rnd2, p + 1)
                        dve.scalar_tensor_tensor(s2[j][64:S_ROWS, :], f32(rnd2[64:S_ROWS, :]),
                                                 c_sb[64:S_ROWS, C_MS2:C_MS2 + 1], bank[0][64:S_ROWS, 0:C],
                                                 ALU.mult, ALU.add).then_inc(b_s2, 1)
                    if ln and v == 7:
                        norm_b(p + 1)

            def step_b_tail(p, j, old2, old, new, ln):
                if isinstance(p, int) and p == PAIRS + 1:
                    residual(p - 2, 1)
                else:
                    step_b(p, j, old2, old, new, ln)

            steps(dve, step_b_tail, BODY_B)

            def norm_c(p):
                norm(p, c_ln, c_inv, 2, 1, c_hn, hn_all, lambda c: ds(p * CH + c, 1))

            def gates(p, part):
                n = [GATE * p + (0 if part == 0 else GATE_D)]

                def done(ins):
                    n[0] = n[0] + 1
                    ins.then_inc(c_gate, 1)
                    dve.wait_ge(c_gate, n[0])

                def wide(t):
                    return t.unsqueeze(2).to_broadcast([T, CH, E])

                dsc = desc[:, :].unsqueeze(1).to_broadcast([T, CH, E])
                if part == 0:
                    done(dve.tensor_tensor(lg[:, 0, :, :], bank[1][0:T, 0:CH * E].rearrange("p (c e) -> p c e", c=CH),
                                           gb_sb[:, :].unsqueeze(1).to_broadcast([T, CH, E]), ALU.add))
                    for k in range(2):
                        src = lg[:, 3 * k, :, :]
                        done(dve.tensor_reduce(top[:, 2 * k, :], src, AX.X, ALU.max))
                        done(dve.tensor_tensor(lg[:, 1, :, :], src, wide(top[:, 2 * k, :]), ALU.is_equal))
                        done(dve.tensor_tensor(lg[:, 5, :, :], lg[:, 1, :, :], dsc, ALU.mult))
                        done(dve.tensor_reduce(top[:, 2 * k + 1, :], lg[:, 5, :, :], AX.X, ALU.max))
                        done(dve.tensor_tensor(lg[:, 2 + 2 * k, :, :], lg[:, 5, :, :], wide(top[:, 2 * k + 1, :]),
                                               ALU.is_equal))
                        if k == 0:
                            done(dve.scalar_tensor_tensor(lg[:, 3, :, :], lg[:, 2, :, :], -BIG, lg[:, 0, :, :],
                                                          ALU.mult, ALU.add))
                    done(dve.tensor_tensor(top[:, 6, :], top[:, 2, :], top[:, 0, :], ALU.subtract))
                else:
                    dve.wait_ge(c_e, p + 1)
                    done(dve.tensor_scalar(top[:, 8, :], top[:, 7, :], 1.0, None, ALU.add))
                    done(dve.reciprocal(top[:, 9, :], top[:, 8, :]))
                    done(dve.tensor_tensor(top[:, 10, :], top[:, 9, :], top[:, 7, :], ALU.mult))
                    dve.tensor_tensor(lg[:, 5, :, :], lg[:, 2, :, :], wide(top[:, 9, :]), ALU.mult)
                    done(dve.tensor_tensor(lg[:, 6, :, :], lg[:, 4, :, :], wide(top[:, 10, :]), ALU.mult))
                    wait(dve, c_wtt, p)
                    dve.tensor_tensor(wtok[:, :, 0:E], lg[:, 5, :, :], lg[:, 6, :, :], ALU.add)
                    done(dve.tensor_tensor(wtok[:, :, 32:32 + E], lg[:, 5, :, :], lg[:, 6, :, :], ALU.add))

            def result(p):
                dve.wait_ge(c_f, p + 1)
                dve.tensor_tensor(yt[:, :, :], bank[1][0:T, 0:CH * D].rearrange("p (c d) -> p c d", c=CH),
                                  hn_all[:, ds(p * CH, CH), :], ALU.add).then_inc(c_fin, 1)
                dve.wait_ge(c_fin, 4 * p + 1)
                for c in range(CH):
                    last = dve.bn_stats(stats2[:, c, :], yt[:, c, :])
                last.then_inc(c_fin, 1)
                dve.wait_ge(c_fin, 4 * p + 2)
                dve.memset(spare[:, :], 0.0)
                for c in range(CH):
                    last = dve.bn_aggr(aggr2[:, c, :], stats2[:, c, :])
                last.then_inc(c_fin, 1)
                dve.wait_ge(c_fin, 4 * p + 3)

            def result2(p):
                dve.wait_ge(c_pinv, 2 * p + 2)
                wait(dve, c_gres, 2 * p)
                for c in range(CH):
                    last = dve.tensor_scalar(yz[:, 0, c, :], yt[:, c, :], aggr2[:, c, 0:1], inv2[:, 1, c:c + 1],
                                             ALU.subtract, ALU.mult)
                last.then_inc(c_fin, 1)

            def step_c(p, j, old2, old, new, ln):
                if isinstance(p, int) and p == 0:
                    dve.wait_ge(b_res, 2 * PAIRS)
                    norm_c(0)
                for v in range(8):
                    if old:
                        for e in (2 * v, 2 * v + 1):
                            dve.wait_ge(c_relu, 16 * (p - 1) + e + 1)
                            dve.wait_ge(c_wb, 16 * (p - 1) + e + 1)
                            wait(dve, c_dn, 8 * (p - 1) + v - 1)
                            dve.tensor_tensor(gated[e % 4][:, :], relu_sb[e % 2][:, :], bank[4 + e % 2][:, 0:C],
                                              ALU.mult).then_inc(c_gated, 1)
                    if new and v == 0:
                        dve.wait_ge(c_rnd, p + 1)
                        wait(dve, c_up, 16 * (p - 1))
                        dve.scalar_tensor_tensor(s1[j][:, :], f32(rnd1[:, :]), c_sb[:, C_MS1:C_MS1 + 1],
                                                 bank[0][:, 0:C], ALU.mult, ALU.add).then_inc(c_s1, 1)
                    if old2 and v == 1:
                        result(p - 2)
                    if new and v == 2:
                        dve.wait_ge(c_lg, p + 1)
                        gates(p, 0)
                    if old2 and v == 3:
                        result2(p - 2)
                    if new and v == 4:
                        gates(p, 1)
                    if new and v == 5:
                        dve.wait_ge(c_rndw, p + 1)
                        wait(dve, c_wb, 16 * (p - 1))
                        dve.scalar_tensor_tensor(wt[j][:, :], f32(rnd2[0:48, :]), c_sb[0:48, C_MG:C_MG + 1],
                                                 bank[0][0:48, 0:C], ALU.mult, ALU.add).then_inc(c_wt, 1)
                    if ln and v == 6:
                        norm_c(p + 1)

            steps(dve, step_c, BODY_C)

        @block.tensor
        def _(pe):
            pe.wait_ge(ld_a, 16 * len(A_LOADS))
            for h in range(H):
                pe.matmul(bank[6][:, h * D:(h + 1) * D], wqT_sb[:, h, :], wkT_sb[:, h, :], start=True, stop=True)
                last = pe.matmul(bank[7][:, h * D:(h + 1) * D], wvT_sb[:, h, :], woT_sb[:, h, :],
                                 start=True, stop=True)
            last.then_inc(s_wprod, 1)
            pe.wait_ge(s_prep, PREP_W)
            pe.wait_ge(s_prepg, PREP_GA)

            with pe.Fori(0, PAIRS // CHAINS) as i:
                for k in range(STEPS):
                    for j in range(CHAINS):
                        if k == 0:
                            pe.wait_ge(a_x, i * CHAINS + j + 1)
                            pe.wait_ge(a_h, i * CHAINS + 1)
                        else:
                            pe.wait_ge(a_st[j], (i * STEPS + k) * 2)
                        last = pe.matmul(bank[j][:, 0:C], aw[:, :], x_st[j][:, :], start=True, stop=k == 0)
                        if k:
                            last = pe.matmul(bank[j][:, 0:C].rearrange("p (b l) -> p b l", b=2), w2bd_sb[:, :],
                                             state[j][:, :, 0:L], start=False, stop=True)
                        last.then_inc(a_mm[j], 1)
                for j in range(CHAINS):
                    pe.wait_ge(a_st[j], (i * STEPS + STEPS) * 2)
                    pe.matmul(bank[4 + j][:, 0:C], cw[:, :], x_st[j][:, :], start=True, stop=False)
                    pe.matmul(bank[4 + j][:, 0:C].rearrange("p (b l) -> p b l", b=2), w4_sb[:, :],
                              shifted[j][:, :, :], start=False, stop=True).then_inc(a_c, 1)
                for j in range(CHAINS):
                    pe.wait_ge((a_miu0, a_miu1)[j % 2], i * 2 + j // 2 + 1)
                    for c in range(CH):
                        last = pe.transpose(bank[j][0:T, c * 128:(c + 1) * 128], miu[j][:, c * T:(c + 1) * T], ident)
                    last.then_inc(a_t, 1)

            def products(p, v, jj):
                b = v // 4
                pe.wait_ge(b_cap, 16 * p + 2 * v + 2)
                if v % 4 == 0:
                    wait(pe, b_y, 2 * p + b)
                for hh in range(2):
                    h = (2 * v + hh) % H
                    for c in range(2):
                        last = pe.matmul(bank[1][64 * c:64 * c + 64, 0:L], u_sb[jj][:, 2 * b + c, h * D:(h + 1) * D],
                                         prob[(2 * v + c) % 4][:, hh, :], start=h == 0, stop=h == H - 1)
                last.then_inc(b_pv, 1)

            def fold_b(p, b):
                pe.wait_ge(b_y, 2 * p + b + 1)
                for c in range(2):
                    last = pe.matmul(bank[0][0:T, c * D:(c + 1) * D], y_att[:, c * T:(c + 1) * T], fold,
                                     start=True, stop=True)
                last.then_inc(b_f, 1)

            def step_b(p, j, old2, old, new, ln):
                o = 1 - j
                for v in range(8):
                    if old:
                        b, hp = v // 4, v % 4
                        if v == 0:
                            pe.wait_ge(b_row, 32 * p)
                            pe.wait_ge(b_gl, 8 * p)
                        for c in range(2):
                            n = 2 * v + c
                            wait(pe, b_exp, 16 * (p - 1) + n - 3)
                            cols = slice((2 * b + c) * T, (2 * b + c + 1) * T)
                            ps = bank[4 + n % 4][0:T, 0:C].rearrange("p (h l) -> p h l", h=2)
                            pe.matmul(ps, s1[o][:, cols], m1[o][:, 2 * hp:2 * hp + 2, b * L:(b + 1) * L],
                                      start=True, stop=False)
                            pe.matmul(ps, s2[o][:, cols], m2[o][:, 2 * hp:2 * hp + 2, b * L:(b + 1) * L],
                                      start=False, stop=True).then_inc(b_sc, 1)
                    if v == 0 and old2:
                        products(p - 2, 7, j)
                    if v > 0 and old:
                        products(p - 1, v - 1, o)
                    if new and v == 0:
                        pe.wait_ge(b_xn, p + 1)
                        wait(pe, b_s2, p)
                        wait(pe, b_res, 2 * (p - 1) - 1)
                        for c in range(CH):
                            last = pe.transpose(bank[0][:, c * T:(c + 1) * T],
                                                xn[:, c, :, :].rearrange("p a d -> p (a d)"), ident[0:T, 0:T])
                        last.then_inc(b_xt, 1)
                    if old2 and v == 1:
                        if new:
                            pe.wait_ge(b_s1, p + 1)
                            pe.wait_ge(b_rnd, 2 * p + 2)
                        fold_b(p - 2, 1)
                    if new and 1 <= v <= 4:
                        c = v - 1
                        if c == 0:
                            pe.wait_ge(b_s1, p + 1)
                            pe.wait_ge(b_rnd, 2 * p + 2)
                        for q in range(3):
                            n = 3 * c + q
                            if n < 2:
                                wait(pe, b_gl, 8 * (p - 1) + 7 + n)
                            else:
                                pe.wait_ge(b_ev, 20 * p + n - 1)
                            for w, first in ((wqku_hi, True), (wqku_lo, False)):
                                last = pe.matmul(bank[2 + n % 2][0:T, :], s1[j][:, c * T:(c + 1) * T], w[:, q, :],
                                                 start=first, stop=not first)
                            last.then_inc(b_pj, 1)
                    if new and v >= 5:
                        for h in range(3 * (v - 5), min(3 * (v - 5) + 3, H)):
                            if h < 2:
                                pe.wait_ge(b_ev, 20 * p + 11 + h)
                            else:
                                pe.wait_ge(b_gl, 8 * p + h - 1)
                            for w, first in ((wg_hi, True), (wg_lo, False)):
                                last = pe.matmul(bank[2 + h % 2][:, 0:C], w[:, h, :, :].rearrange("p a d -> p (a d)"),
                                                 s1[j][:, :], start=first, stop=not first)
                            last.then_inc(b_pj, 1)
                    if old and v == 5:
                        wait(pe, b_res, 2 * (p - 1))
                        fold_b(p - 1, 0)
                    if new and v == 6:
                        pe.wait_ge(b_qkw, 2 * p + 2)
                        wait(pe, b_res, 2 * (p - 1) + 1)
                        for c in range(CH):
                            last = pe.transpose(bank[0][0:S_ROWS, c * T:(c + 1) * T], qkw[:, c, :], ident[0:T, 0:T])
                        last.then_inc(b_qt, 1)

            def step_b_tail(p, j, old2, old, new, ln):
                if isinstance(p, int) and p == PAIRS + 1:
                    products(p - 2, 7, j)
                    wait(pe, b_res, 2 * (p - 1) - 1)
                    fold_b(p - 2, 1)
                else:
                    step_b(p, j, old2, old, new, ln)

            pe.wait_ge(s_prepg, PREP_G)
            pe.wait_ge(a_h, PAIRS + 1)
            steps(pe, step_b_tail, BODY_B)

            def down(p, v, jj):
                y = bank[6 + jj]
                if v == 0:
                    wait(pe, c_y, p - 1)
                    pe.matmul(y[:, 0:C], b2_hi[:, :], wt[jj][:, :], start=True, stop=False, skip_group_check=True)
                    pe.matmul(y[:, 0:C], b2_lo[:, :], wt[jj][:, :], start=False, stop=False, skip_group_check=True)
                pe.wait_ge(c_gated, 16 * p + 2 * v + 2)
                for k in range(2):
                    e = 2 * v + k
                    last = pe.matmul(y[64 * k:64 * k + 64, 0:C], w2_sb[:, e, :], gated[e % 4][:, :],
                                     start=False, stop=v == 7, skip_group_check=True)
                last.then_inc(c_dn, 1)

            def step_c(p, j, old2, old, new, ln):
                o = 1 - j
                for v in range(8):
                    if old:
                        for e in (2 * v, 2 * v + 1):
                            wait(pe, c_relu, 16 * (p - 1) + e - 1)
                            for w, first in ((w1_hi, True), (w1_lo, False)):
                                last = pe.matmul(bank[2 + e % 2][:, 0:C], w[:, e, :], s1[o][:, :],
                                                 start=first, stop=not first)
                            last.then_inc(c_up, 1)
                            if e == 0:
                                pe.wait_ge(c_wt, p)
                            wait(pe, c_gated, 16 * (p - 1) + e - 1)
                            pe.matmul(bank[4 + e % 2][:, 0:C], sel[:, e, :], wt[o][:, :], start=True, stop=True)\
                                .then_inc(c_wb, 1)
                    if v == 0 and old2:
                        down(p - 2, 7, j)
                    if v > 0 and old:
                        down(p - 1, v - 1, o)
                    if new and v == 0:
                        pe.wait_ge(c_xn, p + 1)
                        wait(pe, c_wt, p)
                        for c in range(CH):
                            last = pe.transpose(bank[0][:, c * T:(c + 1) * T],
                                                xn[:, c, :, :].rearrange("p a d -> p (a d)"), ident[0:T, 0:T])
                        last.then_inc(c_xt, 1)
                    if old2 and v == 1:
                        pe.wait_ge(c_y, p - 1)
                        wait(pe, c_gate, GATE * (p if new else PAIRS))
                        for c in range(CH):
                            last = pe.matmul(bank[1][0:T, c * D:(c + 1) * D], y_moe[:, c * T:(c + 1) * T], fold,
                                             start=True, stop=True)
                        last.then_inc(c_f, 1)
                    if new and v == 2:
                        pe.wait_ge(c_s1, p + 1)
                        wait(pe, c_fin, 4 * (p - 2) + 1)
                        for c in range(CH):
                            for w, first in ((gw_hi, True), (gw_lo, False)):
                                last = pe.matmul(bank[1][0:T, c * E:(c + 1) * E], s1[j][:, c * T:(c + 1) * T], w[:, :],
                                                 start=first, stop=not first)
                        last.then_inc(c_lg, 1)
                    if new and v == 5:
                        pe.wait_ge(c_gate, GATE * (p + 1))
                        for c in range(CH):
                            last = pe.transpose(bank[0][0:W_ROWS, c * T:(c + 1) * T], wtok[:, c, :], ident[0:T, 0:T])
                        last.then_inc(c_wtt, 1)

            pe.wait_ge(b_res, 2 * PAIRS)
            steps(pe, step_c, BODY_C)


PREP_A = 4
PREP_W = 7
PREP_GA = 3 * CHAINS
PREP_G = PREP_GA + 29
GATE_D = 13
GATE = GATE_D + 5


def kernel(**inputs):
    import concourse.bacc as bacc
    from concourse.bass_utils import run_bass_kernel_spmd

    def a(name):
        return np.asarray(inputs[name])

    def rows(x, n):
        return np.broadcast_to(x[None], (n,) + x.shape)

    def stacked(w, rev_left, rev_right, fwd_left, fwd_right, bias):
        o = np.zeros((AROWS, 128), np.float32)
        for g in range(4):
            f = slice(g * D_IN, (g + 1) * D_IN)
            r = slice(XROWS + g * D_IN, XROWS + (g + 1) * D_IN)
            for half, fwd, rev in ((0, fwd_left, rev_left), (1, fwd_right, rev_right)):
                cols = slice(half * D, half * D + D)
                if fwd:
                    o[f, cols] = w.T
                if rev:
                    o[r, cols] = w.T
        o[AROWS - 2:, :] = np.concatenate([bias, bias])
        return o

    def bias_rows(b):
        o = np.zeros((AROWS, 128), np.float32)
        o[AROWS - 2:, :] = np.concatenate([b, b])
        return o

    x = a("x").reshape(PAIRS, 2, D_IN, L).transpose(0, 2, 1, 3)
    xr = np.concatenate([np.tile(x, (1, 4, 1, 1)), np.tile(x[..., ::-1], (1, 4, 1, 1))], axis=1)
    W2T, W4T = a("L0_tok_W2").T, a("L0_tok_W4").T
    w2bd = np.zeros((128, 128), np.float32)
    w2bd[:D, :D] = W2T
    w2bd[D:, D:] = W2T
    w_q, w_k, w_v = a("L0_attn_W_q"), a("L0_attn_W_k"), a("L0_attn_W_v")
    qT, kT, vT = (w.transpose(2, 0, 1) for w in (w_q, w_k, w_v))
    oT = a("L0_attn_W_o").reshape(D, H, D).transpose(2, 1, 0)
    b2 = np.zeros((48, 128), np.float32)
    b2[0:E, 0:D] = b2[32:32 + E, 0:D] = a("L0_ffn_b2")
    arrays = {
        "cst": constants(),
        "xr": xr.reshape(PAIRS, 2 * XROWS, C),
        "aw1": stacked(a("L0_tok_W1"), False, True, True, False, a("L0_tok_b1")),
        "aw2": bias_rows(a("L0_tok_b2")),
        "cw1": stacked(a("L0_tok_W3"), False, False, True, True, a("L0_tok_b3")),
        "cw2": bias_rows(a("L0_tok_b4")),
        "w2bd": w2bd,
        "w4dup": np.tile(W4T, (2, 2)),
        "wqT": np.concatenate([qT, qT], axis=2),
        "wkT": kT,
        "wvT": np.concatenate([vT, vT], axis=2),
        "woT": oT,
        "wq": np.tile(w_q.transpose(1, 0, 2).reshape(D, H * D), (2, 1)),
        "wk": np.tile(w_k.transpose(1, 0, 2).reshape(D, H * D), (2, 1)),
        "gam": rows(a("L0_attn_gamma").reshape(H), 128),
        "lns": rows(a("L0_attn_ln_scale"), T),
        "gw": np.tile(a("L0_ffn_gate_w"), (2, 1)),
        "gb": rows(a("L0_ffn_gate_b"), T),
        "w1": np.tile(a("L0_ffn_w1").transpose(1, 0, 2), (2, 1, 1)),
        "b1": a("L0_ffn_b1").T,
        "w2": a("L0_ffn_w2").transpose(1, 0, 2),
        "b2": b2,
        "fg": rows(a("L0_ffn_gamma"), T),
        "fb": rows(a("L0_ffn_beta"), T),
    }
    nc = bacc.Bacc("TRN2", target_bir_lowering=False, num_devices=1)
    ins, args = {}, {}
    for name, v in arrays.items():
        v = np.ascontiguousarray(v)
        ins[f"in_{name}"] = v
        args[name] = nc.dram_tensor(f"in_{name}", v.shape, mybir.dt.from_np(v.dtype), kind="ExternalInput").ap()
    out = nc.dram_tensor("out", (B, L, D), F32, kind="ExternalOutput").ap()
    build(nc, **args, out=out)
    r = run_bass_kernel_spmd(nc, [ins], core_ids=[0])
    return r.results[0]["out"]
```

```python
from contextlib import ExitStack

import numpy as np

import concourse.bass as bass
from concourse import mybir

ALU = mybir.AluOpType
ACT = mybir.ActivationFunctionType
AX = mybir.AxisListType
F32 = mybir.dt.float32
F32R = mybir.dt.float32r
ds = bass.ds

B, D_IN, L = 32, 4, 250
D = 64
H = 8
E = 16
F = 128
G = 16
R = 128 // E
STEPS = 8
T = L // 2
PAIRS = B // 2
C = 2 * L
CH = 4
NCHUNK = PAIRS * CH
CHAINS = 4
EPS = 1e-5
BIG = 3.0e38

XROWS = 4 * D_IN
AROWS = 2 * XROWS + 2
Q_ROW, ONE_ROW, K_ROW, S_ROWS = 64, 80, 96, 112

W_ROWS = 96

C_IDENT, C_SEL = 0, 128
C_MX, C_MW, C_MS1, C_MS2, C_MG = 256, 257, 258, 259, 260
C_IND = 261
C_COLS = C_IND + H


def constants():
    c = np.zeros((128, C_COLS), np.float32)
    c[:, C_IDENT:C_IDENT + 128] = np.eye(128)
    for half in range(2):
        for g in range(4):
            rows = slice(half * XROWS + g * D_IN, half * XROWS + (g + 1) * D_IN)
            c[rows, C_MX] = -1.0 if g >= 2 else 0.0
            c[rows, C_MW] = -1.0 if g % 2 else 0.0
    c[AROWS - 1, C_MW] = -1.0
    c[64:, C_MS1] = -1.0
    c[Q_ROW + H:Q_ROW + 2 * H, C_MS2] = -1.0
    c[K_ROW + H:K_ROW + 2 * H, C_MS2] = -1.0
    c[32:32 + E, C_MG] = -1.0
    for h in range(H):
        c[K_ROW + h, C_IND + h] = 1.0
        c[K_ROW + H + h, C_IND + h] = 1.0
    for e in range(E):
        c[e, C_SEL + e * R:C_SEL + (e + 1) * R] = 1.0
        c[32 + e, C_SEL + e * R:C_SEL + (e + 1) * R] = 1.0
    return c


def build(nc, cst, xr, aw1, aw2, cw1, cw2, w24, wqT, wkT, wvT, woT, wq, wk, gam, lns,
          gw, gb, w1, b1, w2, b2, fg, fb, out):
    with ExitStack() as ctx:
        def sb(name, shape, dt=F32):
            return ctx.enter_context(nc.sbuf_tensor(name, shape, dt))

        def sem(name):
            return ctx.enter_context(nc.semaphore(name))

        def f32(ap):
            return ap.bitcast(F32)

        bank = [ctx.enter_context(nc.psum_tensor(f"bank{i}", [128, 512], F32)) for i in range(8)]

        c_sb = sb("c_sb", [128, C_COLS])
        ident = c_sb[:, C_IDENT:C_IDENT + 128]
        aw1_sb, aw2_sb = sb("aw1_sb", [AROWS, 128]), sb("aw2_sb", [AROWS, 128])
        cw1_sb, cw2_sb = sb("cw1_sb", [AROWS, 128]), sb("cw2_sb", [AROWS, 128])
        w24_sb = sb("w24_sb", [128, 2, 128])
        gam_sb, lns_sb = sb("gam_sb", [128, H]), sb("lns_sb", [T, D])
        gwraw, gb_sb = sb("gwraw", [128, W_ROWS]), sb("gb_sb", [T, E])
        b1_sb, w2_sb = sb("b1_sb", [128, G]), sb("w2_sb", [128, G, D])
        b2raw = sb("b2raw", [48, 128])
        fg_sb, fb_sb = sb("fg_sb", [T, D]), sb("fb_sb", [T, D])

        aw, cw = sb("aw", [AROWS, 128], F32R), sb("cw", [AROWS, 128], F32R)
        w24_hi, w24_lo = sb("w24_hi", [128, 2, 128], F32R), sb("w24_lo", [128, 2, 128], F32R)
        awt = sb("awt", [AROWS, 2, 128])
        awr = sb("awr", [AROWS, 2, 128], F32R)
        wqku_hi = sb("wqku_hi", [128, 3, H * D], F32R)
        wqku_lo = sb("wqku_lo", [128, 3, H * D], F32R)
        wg_hi, wg_lo = sb("wg_hi", [128, H, 2, D], F32R), sb("wg_lo", [128, H, 2, D], F32R)
        gw_hi, gw_lo = sb("gw_hi", [128, W_ROWS], F32R), sb("gw_lo", [128, W_ROWS], F32R)
        w1_hi, w1_lo = sb("w1_hi", [128, G, 128], F32R), sb("w1_lo", [128, G, 128], F32R)
        b2_hi, b2_lo = sb("b2_hi", [48, 128], F32R), sb("b2_lo", [48, 128], F32R)
        sel = sb("sel", [48, 128], F32R)
        g2 = sb("g2", [128, H])
        gneg = sb("gneg", [128, H])
        cap_lo, cap_hi = sb("cap_lo", [128, H]), sb("cap_hi", [128, H])
        spare, spare2 = sb("spare", [T, 1]), sb("spare2", [T, 1])
        mhalf, eps = sb("mhalf", [T, CH]), sb("eps", [T, CH])

        h_all = sb("h_all", [T, NCHUNK, D])

        stats, aggr = sb("stats", [T, CH, 6]), sb("aggr", [T, CH, 2])
        inv = sb("inv", [T, 8, CH])
        z, z2 = sb("z", [T, CH, D]), sb("z2", [T, 2, D])
        xn = sb("xn", [T, CH, 2, D])
        rnd1, rnd2 = sb("rnd1", [128, C], F32R), sb("rnd2", [128, C], F32R)
        s1 = [sb(f"s1_{j}", [128, C], F32R) for j in range(2)]
        m2 = [sb(f"m2_{j}", [S_ROWS, H, C], F32R) for j in range(2)]
        qk = sb("qk", [T, CH, 2, H])
        qkw = sb("qkw", [T, CH, S_ROWS])

        lg = sb("lg", [T, 8, CH, E])
        top = sb("top", [T, 12, CH])
        desc = sb("desc", [T, E])
        wtok = sb("wtok", [T, CH, W_ROWS])

        def phase(*tensors):
            with ExitStack() as scope:
                return [[scope.enter_context(nc.sbuf_tensor(f"{name}{j}", shape, dt)) for j in range(n)]
                        for name, n, shape, dt in tensors]

        x_raw, x_rnd, x_st, st_hi, st_lo, sh_hi, sh_lo, miu, (wqT_sb,), (wkT_sb,), (wvT_sb,), (woT_sb,), (wraw,), (w1raw,) = phase(
            ("x_raw", CHAINS, [2 * XROWS, C], F32), ("x_rnd", 2, [2 * XROWS, C], F32R),
            ("x_st", CHAINS, [AROWS, C], F32R),
            ("st_hi", CHAINS, [128, 2, L + 1], F32R), ("st_lo", CHAINS, [128, 2, L + 1], F32R),
            ("sh_hi", CHAINS, [128, 2, L], F32R), ("sh_lo", CHAINS, [128, 2, L], F32R), ("miu", CHAINS, [128, C], F32),
            ("wqT_sb", 1, [64, H, 128], F32), ("wkT_sb", 1, [64, H, 64], F32),
            ("wvT_sb", 1, [64, H, 128], F32), ("woT_sb", 1, [64, H, 64], F32),
            ("wraw", 1, [128, 4, H * D], F32), ("w1raw", 1, [128, G, 128], F32))
        m1, s2, u_sb, sq, prob, (y_att,) = phase(
            ("m1_", 2, [128, H, C], F32R), ("s2_", 2, [S_ROWS, C], F32R), ("u", 2, [T, CH, H * D], F32), ("sq", 2, [T, H * D], F32),
            ("prob", 4, [T, 2, L], F32), ("y_att", 1, [128, L], F32))
        relu_sb, gated, (y_moe,), (yt,), (yt2,), (stats2,), (aggr2,), (inv2,), (yz,), (res,), (hn_all,), (lgt,), wb, wt = phase(
            ("relu", 4, [128, C], F32), ("gated", 8, [128, C], F32), ("y_moe", 1, [128, C], F32),
            ("yt", 1, [T, CH, D], F32), ("yt2_", 1, [T, CH, D], F32), ("stats2_", 1, [T, CH, 6], F32), ("aggr2_", 1, [T, CH, 2], F32),
            ("inv2_", 1, [T, 4, CH], F32), ("yz", 1, [T, 3, CH, D], F32), ("res", 1, [T, CH, D], F32),
            ("hn_all", 1, [T, NCHUNK, D], F32),
            ("lgt", 1, [W_ROWS, C], F32), ("wb", 2, [128, C], F32), ("wt", 2, [48, C], F32R))

        ld_a, ld_b, ld_c = sem("ld_a"), sem("ld_b"), sem("ld_c")
        s_prep = sem("s_prep")
        s_prepg = sem("s_prepg")
        s_wprod = sem("s_wprod")
        a_xin = [sem(f"a_xin{j}") for j in range(CHAINS)]
        a_rnd, a_x = sem("a_rnd"), sem("a_x")
        a_mm = [sem(f"a_mm{j}") for j in range(CHAINS)]
        a_hi = [sem(f"a_hi{j}") for j in range(CHAINS)]
        a_lo = [sem(f"a_lo{j}") for j in range(CHAINS)]
        a_c, a_miu0, a_miu1, a_t, a_h = (sem(n) for n in ("a_c", "a_miu0", "a_miu1", "a_t", "a_h"))
        b_ln, b_inv, b_z, b_xn = (sem(n) for n in ("b_ln", "b_inv", "b_z", "b_xn"))
        b_xt, b_rnd, b_s1 = sem("b_xt"), sem("b_rnd"), sem("b_s1")
        b_pj, b_ev, b_red, b_gl = sem("b_pj"), sem("b_ev"), sem("b_red"), sem("b_gl")
        b_qkw, b_qt, b_rnd2, b_s2, b_row = (sem(n) for n in ("b_qkw", "b_qt", "b_rnd2", "b_s2", "b_row"))
        b_sc, b_exp, b_cap, b_pv = sem("b_sc"), sem("b_exp"), sem("b_cap"), sem("b_pv")
        b_y, b_f, b_half, b_res = sem("b_y"), sem("b_f"), sem("b_half"), sem("b_res")
        c_ln, c_inv, c_hn, c_xn = (sem(n) for n in ("c_ln", "c_inv", "c_hn", "c_xn"))
        c_xt, c_rnd, c_s1, c_lgt, c_lgs, c_lg = (sem(n) for n in ("c_xt", "c_rnd", "c_s1", "c_lgt", "c_lgs", "c_lg"))
        c_gate, c_e, c_wtt, c_rndw, c_wt = (sem(n) for n in ("c_gate", "c_e", "c_wtt", "c_rndw", "c_wt"))
        c_up, c_wb, c_wbs, c_relu, c_gated, c_dn = (
            sem(n) for n in ("c_up", "c_wb", "c_wbs", "c_relu", "c_gated", "c_dn"))
        c_y, c_f, c_half, c_fin, c_pinv, c_gres, c_pout, c_out = (
            sem(n) for n in ("c_y", "c_f", "c_half", "c_fin", "c_pinv", "c_gres", "c_pout", "c_out"))

        def wait(eng, s, value):
            if not (isinstance(value, int) and value <= 0):
                eng.wait_ge(s, value)

        A_LOADS = [(c_sb, cst), (aw1_sb, aw1), (aw2_sb, aw2), (cw1_sb, cw1), (cw2_sb, cw2),
                   (w24_sb, w24), (gam_sb, gam), (wqT_sb, wqT), (wkT_sb, wkT),
                   (wvT_sb, wvT), (woT_sb, woT)]
        B_LOADS = [(wraw[:, 0, :], wq), (wraw[:, 1, :], wk), (lns_sb, lns), (gwraw, gw), (gb_sb, gb),
                   (w1raw, w1), (b1_sb, b1), (w2_sb, w2), (b2raw, b2), (fg_sb, fg), (fb_sb, fb)]

        BODY_B = (3, PAIRS - 1)
        BODY_C = (3, PAIRS - 1)

        def steps(eng, step, body):
            first, last = body
            for p in range(first):
                step(p, p % 2, p >= 2, p >= 1, True, True)
            with eng.Fori(0, (last - first) // 2) as i:
                for k in range(2):
                    step(i * 2 + (first + k), (first + k) % 2, True, True, True, True)
            for p in range(last, PAIRS + 2):
                step(p, p % 2, p - 2 < PAIRS, p - 1 < PAIRS, p < PAIRS, p + 1 < PAIRS)

        def units(v):
            return range(3 * (v - 1), min(3 * v, 20)) if v else range(0)

        block = ctx.enter_context(nc.Block())

        @block.sync
        def _(sp):
            def full(t):
                return t[tuple(slice(None) for _ in t.shape)]

            for dst, src in A_LOADS:
                sp.dma_start(full(dst), full(src)).then_inc(ld_a, 16)
            for j in range(CHAINS):
                sp.dma_start(x_raw[j][:, :], xr[j, :, :]).then_inc(a_xin[j], 16)
            for dst, src in B_LOADS:
                sp.dma_start(full(dst), full(src)).then_inc(ld_b, 16)

            with sp.Fori(1, PAIRS // CHAINS) as i:
                for j in range(CHAINS):
                    sp.wait_ge(a_x, i * CHAINS - (CHAINS - 1 - j))
                    sp.dma_start(x_raw[j][:, :], xr[ds(i * CHAINS + j, 1), :, :].rearrange("a r c -> (a r) c"))\
                        .then_inc(a_xin[j], 16)

            def step_b(p, j, old2, old, new, ln):
                if new:
                    sp.wait_ge(b_s2, p + 1)
                    wait(sp, b_sc, 16 * (p - 1))
                    for k in range(2):
                        sp.dma_start(f32(m2[j][ONE_ROW + k:ONE_ROW + k + 1, :, :]),
                                     f32(s2[j][Q_ROW + k * H:Q_ROW + (k + 1) * H, :])).then_inc(b_row, 16)

            steps(sp, step_b, BODY_B)

            with sp.Fori(0, PAIRS) as i:
                sp.wait_ge(c_pout, i + 1)
                sp.dma_start(out[ds(i * 2, 2), :, :].rearrange("b (k t) d -> t (b k) d", k=2), res[:, :, :])\
                    .then_inc(c_out, 16)
            sp.wait_ge(c_out, 16 * PAIRS)

        @block.gpsimd
        def _(gp):
            count = [0]

            def done(ins):
                count[0] += 1
                ins.then_inc(s_prepg, 1)
                gp.wait_ge(s_prepg, count[0])

            for j in range(CHAINS):
                for t in (st_hi[j], st_lo[j], sh_hi[j], sh_lo[j]):
                    done(gp.memset(f32(t[:, :, :]), 0.0))
                done(gp.memset(f32(x_st[j][32:34, :]), 1.0))
            for j in range(2):
                done(gp.memset(f32(m2[j][64:96, :, :]), 0.0))
            done(gp.memset(qkw[:, :, :], 0.0))
            done(gp.memset(wtok[:, :, :], 0.0))
            for counter in (a_c, a_h):
                gp.memset(spare2[:, :], 0.0).then_inc(counter, 1)
                gp.wait_ge(counter, 1)
            done(gp.memset(eps[:, :], EPS))
            done(gp.memset(mhalf[:, :], -0.5))
            done(gp.memset(qkw[:, :, ONE_ROW:ONE_ROW + 2], 1.0))
            done(gp.iota(lg[:, 7, 0, :].bitcast(mybir.dt.int32), [[-1, E]], base=E, channel_multiplier=0))
            done(gp.tensor_copy(desc[:, :], lg[:, 7, 0, :].bitcast(mybir.dt.int32)))

            gp.wait_ge(ld_a, 16 * len(A_LOADS))
            gp.wait_ge(ld_b, 16 * len(B_LOADS))
            for j in range(2):
                done(gp.tensor_copy(m2[j][K_ROW:S_ROWS, :, :],
                                    c_sb[K_ROW:S_ROWS, C_IND:C_IND + H].unsqueeze(2).to_broadcast([2 * H, H, C])))
            done(gp.tensor_copy(sel[:, :], c_sb[0:48, C_SEL:C_SEL + 128]))
            gp.wait_ge(s_prep, PREP_W)
            for q, src in ((0, 0), (1, 1), (2, 3)):
                done(gp.tensor_copy(wqku_hi[:, q, :], wraw[:, src, :]))
            graw = wraw[:, 2, :].rearrange("p (h d) -> p h d", h=H)
            for k in range(2):
                done(gp.tensor_copy(wg_hi[:, :, k, :], graw))
            done(gp.tensor_copy(gw_hi[:, :], gwraw[:, :]))
            done(gp.tensor_copy(b2_hi[:, :], b2raw[:, :]))
            done(gp.tensor_copy(w1_hi[:, :, :], w1raw[:, :, :]))
            for q, src in ((0, 0), (1, 1), (2, 3)):
                done(gp.tensor_tensor(wqku_lo[:, q, :], wraw[:, src, :], f32(wqku_hi[:, q, :]), ALU.subtract))
            for k in range(2):
                done(gp.tensor_tensor(wg_lo[:, :, k, :], graw, f32(wg_hi[:, :, k, :]), ALU.subtract))
            done(gp.tensor_tensor(gw_lo[:, :], gwraw[:, :], f32(gw_hi[:, :]), ALU.subtract))
            done(gp.tensor_tensor(b2_lo[:, :], b2raw[:, :], f32(b2_hi[:, :]), ALU.subtract))
            done(gp.tensor_tensor(w1_lo[:, :, :], w1raw[:, :, :], f32(w1_hi[:, :, :]), ALU.subtract))
            assert count[0] == PREP_G

            lns4 = lns_sb[:, :].unsqueeze(1).unsqueeze(1).to_broadcast([T, CH, 2, D])
            gneg4 = gneg[0:T, :].unsqueeze(1).unsqueeze(1).to_broadcast([T, CH, 2, H])

            def b_scales(p):
                n = 7 * p
                gp.wait_ge(b_ln, 2 * p + 2)
                wait(gp, b_z, p)
                var = aggr[:, :, 1]
                gp.tensor_tensor(inv[:, 0, :], var, eps[:, :], ALU.add).then_inc(b_inv, 1)
                gp.wait_ge(b_inv, n + 1)
                gp.tensor_tensor(inv[:, 1, :], inv[:, 0, :], mhalf[:, :], ALU.pow).then_inc(b_inv, 1)
                gp.wait_ge(b_inv, n + 2)
                gp.tensor_tensor(inv[:, 2, :], var, inv[:, 1, :], ALU.mult).then_inc(b_inv, 1)
                gp.wait_ge(b_inv, n + 3)
                gp.tensor_tensor(inv[:, 3, :], inv[:, 2, :], inv[:, 1, :], ALU.mult).then_inc(b_inv, 1)
                gp.wait_ge(b_inv, n + 4)
                gp.tensor_tensor(inv[:, 4, :], inv[:, 3, :], eps[:, :], ALU.add).then_inc(b_inv, 1)
                gp.wait_ge(b_inv, n + 5)
                gp.tensor_tensor(inv[:, 5, :], inv[:, 4, :], mhalf[:, :], ALU.pow).then_inc(b_inv, 1)
                gp.wait_ge(b_inv, n + 6)
                gp.tensor_tensor(inv[:, 6, :], inv[:, 1, :], inv[:, 5, :], ALU.mult).then_inc(b_inv, 1)
                gp.wait_ge(b_z, p + 1)
                wait(gp, b_xt, p)
                gp.tensor_tensor(xn[:, :, :, :], z[:, :, :].unsqueeze(2).to_broadcast([T, CH, 2, D]),
                                 lns4, ALU.mult).then_inc(b_xn, 1)

            def step_b(p, j, old2, old, new, ln):
                if isinstance(p, int) and p == 0:
                    b_scales(0)
                if ln:
                    b_scales(p + 1)
                if new:
                    gp.wait_ge(b_red, 8 * p + 8)
                    wait(gp, b_qt, p)
                    gp.tensor_tensor(
                        qkw[:, :, Q_ROW:Q_ROW + 2 * H].rearrange("p c (a h) -> p c a h", a=2),
                        qk[:, :, 0, :].unsqueeze(2).to_broadcast([T, CH, 2, H]), gneg4, ALU.mult).then_inc(b_qkw, 1)
                    gp.tensor_tensor(
                        qkw[:, :, K_ROW:K_ROW + 2 * H].rearrange("p c (a h) -> p c a h", a=2),
                        qk[:, :, 1, :].unsqueeze(2).to_broadcast([T, CH, 2, H]), gneg4, ALU.mult).then_inc(b_qkw, 1)

            steps(gp, step_b, BODY_B)

            def c_scales(p):
                gp.wait_ge(c_ln, 2 * p + 2)
                wait(gp, c_hn, p)
                gp.tensor_tensor(inv[:, 0, :], aggr[:, :, 1], eps[:, :], ALU.add).then_inc(c_inv, 1)
                gp.wait_ge(c_inv, 2 * p + 1)
                gp.tensor_tensor(inv[:, 1, :], inv[:, 0, :], mhalf[:, :], ALU.pow).then_inc(c_inv, 1)
                gp.wait_ge(c_hn, p + 1)
                wait(gp, c_xt, p)
                gp.tensor_copy(xn[:, :, :, :], hn_all[:, ds(p * CH, CH), :].unsqueeze(2).to_broadcast([T, CH, 2, D]))\
                    .then_inc(c_xn, 1)

            def c_result(p):
                gp.wait_ge(c_fin, 4 * p + 3)
                gp.tensor_tensor(inv2[:, 0, :], aggr2[:, :, 1], eps[:, :], ALU.add).then_inc(c_pinv, 1)
                gp.wait_ge(c_pinv, 2 * p + 1)
                gp.tensor_tensor(inv2[:, 1, :], inv2[:, 0, :], mhalf[:, :], ALU.pow).then_inc(c_pinv, 1)
                gp.wait_ge(c_fin, 4 * p + 4)
                gp.tensor_tensor(yz[:, 1, :, :], yz[:, 0, :, :], fg_sb[:, :].unsqueeze(1).to_broadcast([T, CH, D]),
                                 ALU.mult).then_inc(c_gres, 1)
                gp.wait_ge(c_gres, 2 * p + 1)
                gp.tensor_tensor(yz[:, 2, :, :], yz[:, 1, :, :], fb_sb[:, :].unsqueeze(1).to_broadcast([T, CH, D]),
                                 ALU.add).then_inc(c_gres, 1)
                gp.wait_ge(c_gres, 2 * p + 2)
                wait(gp, c_out, 16 * p)
                gp.tensor_tensor(res[:, :, :], yz[:, 2, :, :], h_all[:, ds(p * CH, CH), :], ALU.add).then_inc(c_pout, 1)

            def step_c(p, j, old2, old, new, ln):
                if isinstance(p, int) and p == 0:
                    c_scales(0)
                if ln:
                    c_scales(p + 1)
                if old2:
                    c_result(p - 2)

            steps(gp, step_c, BODY_C)

        @block.scalar
        def _(act):
            def evac(j, k, i):
                act.wait_ge(a_mm[j], i * STEPS + k + 1)
                ps = bank[j][:, 0:C].rearrange("p (b l) -> p b l", b=2)
                if k < STEPS - 1:
                    act.activation(st_hi[j][:, :, 1:L + 1], ps, ACT.Relu).then_inc(a_hi[j], 2)
                else:
                    act.wait_ge(a_c, i * CHAINS + 1)
                    act.activation(sh_hi[j][0:64, :, 1:L], ps[0:64, :, 0:L - 1], ACT.Relu).then_inc(a_hi[j], 1)
                    act.activation(sh_hi[j][64:128, :, 0:L - 1], ps[64:128, :, L - 2::-1], ACT.Relu)\
                        .then_inc(a_hi[j], 1)

            with act.Fori(0, PAIRS // CHAINS) as i:
                for j in range(CHAINS):
                    act.wait_ge(a_xin[j], i * 16 + 16)
                    if j >= 2:
                        act.wait_ge(a_x, i * CHAINS + j - 1)
                    act.activation(x_rnd[j % 2][:, :], x_raw[j][:, :], ACT.Copy).then_inc(a_rnd, 1)
                for k in range(STEPS):
                    for j in range(CHAINS):
                        evac(j, k, i)
                for j in range(0, CHAINS, 2):
                    act.wait_ge(a_c, i * CHAINS + j + 2)
                    act.activation(miu[j][:, :], bank[4 + j][:, 0:C], ACT.Relu).then_inc(a_miu0, 1)
                for j in range(0, CHAINS, 2):
                    act.wait_ge(a_t, i * CHAINS + j + 1)
                    act.activation(h_all[:, ds(i * CHAINS * CH + j * CH, CH), :],
                                   bank[j][0:T, :].rearrange("p (c d) -> p c d", c=CH)[:, :, 0:D], ACT.Copy)\
                        .then_inc(a_h, 1)

            def evac_y(p, b):
                act.wait_ge(b_pv, 8 * p + 4 * b + 4)
                wait(act, b_f, 2 * p + b)
                act.activation(y_att[:, :], bank[1][:, 0:L], ACT.Copy).then_inc(b_y, 1)

            def step_b(p, j, old2, old, new, ln):
                def exps(v, c):
                    n = 2 * v + c
                    act.wait_ge(b_sc, 16 * (p - 1) + n + 1)
                    wait(act, b_pv, 8 * (p - 1) + v - 1)
                    act.activation(prob[n % 4][:, :, :], bank[4 + n % 4][0:T, 0:C].rearrange("p (h l) -> p h l", h=2),
                                   ACT.Exp).then_inc(b_exp, 1)

                def unit(k):
                    c, q = k // 3, k % 3
                    src = bank[2 + k % 2]
                    act.wait_ge(b_pj, 20 * p + k + 1)
                    if k >= 12:
                        wait(act, b_sc, 16 * (p - 1))
                        act.activation(m1[j][:, k - 12, :], src[:, 0:C], ACT.Copy).then_inc(b_ev, 1)
                    elif q < 2:
                        wait(act, b_red, 8 * p + 2 * c + q - 1)
                        act.activation(sq[q][:, :], src[0:T, :], ACT.Square).then_inc(b_ev, 1)
                    else:
                        wait(act, b_pv, 8 * (p - 1))
                        act.activation(u_sb[j][:, c, :], src[0:T, :], ACT.Copy).then_inc(b_ev, 1)

                for v in range(8):
                    if new and v == 0:
                        act.wait_ge(b_xt, p + 1)
                        wait(act, b_s1, p)
                        act.activation(rnd1[:, :], bank[0][:, 0:C], ACT.Copy).then_inc(b_rnd, 1)
                        wait(act, b_sc, 16 * (p - 1))
                        act.activation(s2[j][0:64, :], bank[0][0:64, 0:C], ACT.Copy).then_inc(b_rnd, 1)
                    rest = list(units(v)) if new else []
                    for c in range(2):
                        if old:
                            exps(v, c)
                        if rest:
                            unit(rest.pop(0))
                    if v == 0 and old2:
                        evac_y(p - 2, 1)
                    if v == 4 and old:
                        evac_y(p - 1, 0)
                    for k in rest:
                        unit(k)
                    if new and v == 5:
                        act.wait_ge(b_qt, p + 1)
                        wait(act, b_s2, p)
                        act.activation(rnd2[64:S_ROWS, :], bank[0][64:S_ROWS, 0:C], ACT.Copy).then_inc(b_rnd2, 1)

            def step_b_tail(p, j, old2, old, new, ln):
                if isinstance(p, int) and p == PAIRS + 1:
                    evac_y(p - 2, 1)
                else:
                    step_b(p, j, old2, old, new, ln)

            steps(act, step_b_tail, BODY_B)

            def round_c(p):
                act.wait_ge(c_xt, p + 1)
                wait(act, c_s1, p)
                act.activation(rnd1[:, :], bank[7][:, 0:C], ACT.Copy).then_inc(c_rnd, 1)

            def step_c(p, j, old2, old, new, ln):
                def relu(g):
                    act.wait_ge(c_up, 16 * (p - 1) + g + 1)
                    wait(act, c_gated, 16 * (p - 1) + g - 3)
                    act.activation(relu_sb[g % 4][:, :], bank[2 + g % 4][:, 0:C], ACT.Relu,
                                   bias=b1_sb[:, g:g + 1]).then_inc(c_relu, 1)

                for v in range(8):
                    if old2 and v == 2:
                        act.wait_ge(c_dn, 8 * (p - 2) + 8)
                        wait(act, c_f, p - 2)
                        act.activation(y_moe[:, :], bank[6][:, 0:C], ACT.Copy).then_inc(c_y, 1)
                    if old:
                        relu(2 * v)
                        relu(2 * v + 1)
                    if old and v == 0:
                        act.wait_ge(c_wb, p)
                        wait(act, c_gated, 16 * (p - 2))
                        act.activation(wb[1 - j][:, :], bank[0][:, 0:C], ACT.Copy).then_inc(c_wbs, 1)
                    if new and v == 0:
                        act.wait_ge(c_lgt, p + 1)
                        wait(act, c_lg, p)
                        act.activation(lgt[:, :], bank[7][0:W_ROWS, 0:C], ACT.Copy).then_inc(c_lgs, 1)
                    if new and v == 5:
                        act.wait_ge(c_gate, GATE * p + GATE_D)
                        act.activation(top[:, 7, :], top[:, 6, :], ACT.Exp).then_inc(c_e, 1)
                    if ln and v == 6:
                        round_c(p + 1)
                    if new and v == 7:
                        act.wait_ge(c_wtt, p + 1)
                        wait(act, c_wt, p)
                        act.activation(rnd2[0:48, :], bank[0][0:48, 0:C], ACT.Copy).then_inc(c_rndw, 1)

            round_c(0)
            steps(act, step_c, BODY_C)

        @block.vector
        def _(dve):
            count = [0]

            def done(ins):
                count[0] += 1
                ins.then_inc(s_prep, 1)
                dve.wait_ge(s_prep, count[0])

            dve.wait_ge(ld_a, 16 * len(A_LOADS))
            done(dve.tensor_tensor(awt[:, 0, :], aw1_sb[:, :], aw2_sb[:, :], ALU.add))
            done(dve.scalar_tensor_tensor(awt[:, 1, :], cw2_sb[:, :], 2.0, cw1_sb[:, :], ALU.mult, ALU.add))
            done(dve.tensor_copy(awr[:, :, :], awt[:, :, :]))
            mw = c_sb[0:AROWS, C_MW:C_MW + 1]
            dve.scalar_tensor_tensor(aw[:, :], f32(awr[:, 0, :]), mw, awt[:, 0, :], ALU.mult, ALU.add)
            done(dve.scalar_tensor_tensor(cw[:, :], f32(awr[:, 1, :]), mw, awt[:, 1, :], ALU.mult, ALU.add))
            done(dve.tensor_copy(w24_hi[:, :, :], w24_sb[:, :, :]))
            done(dve.tensor_tensor(w24_lo[:, :, :], w24_sb[:, :, :], f32(w24_hi[:, :, :]), ALU.subtract))
            assert count[0] == PREP_A
            dve.tensor_scalar(g2[:, :], gam_sb[:, :], 2.0, None, ALU.mult)
            dve.tensor_scalar(gneg[:, :], gam_sb[:, :], -1.0, None, ALU.mult)
            done(dve.tensor_scalar(cap_lo[:, :], gam_sb[:, :], 0.0, None, ALU.is_lt))
            done(dve.tensor_scalar(cap_hi[:, :], cap_lo[:, :], BIG, 1.0, ALU.mult, ALU.add))
            dve.wait_ge(s_wprod, 1)
            dve.tensor_tensor(wraw[:, 2, :].rearrange("p (h d) -> p h d", h=H),
                              bank[6][:, :].rearrange("p (h d) -> p h d", h=H),
                              g2[:, :].unsqueeze(2).to_broadcast([128, H, D]), ALU.mult)
            done(dve.tensor_copy(wraw[:, 3, :], bank[7][:, :]))
            assert count[0] == PREP_W

            def evac(j, k, i):
                dve.wait_ge(a_hi[j], (i * STEPS + k + 1) * 2)
                ps = bank[j][:, 0:C].rearrange("p (b l) -> p b l", b=2)
                if k < STEPS - 1:
                    dve.scalar_tensor_tensor(st_lo[j][:, :, 1:L + 1], ps, 0.0, f32(st_hi[j][:, :, 1:L + 1]),
                                             ALU.max, ALU.subtract).then_inc(a_lo[j], 2)
                else:
                    dve.scalar_tensor_tensor(sh_lo[j][0:64, :, 1:L], ps[0:64, :, 0:L - 1], 0.0,
                                             f32(sh_hi[j][0:64, :, 1:L]), ALU.max, ALU.subtract).then_inc(a_lo[j], 1)
                    dve.scalar_tensor_tensor(sh_lo[j][64:128, :, 0:L - 1], ps[64:128, :, L - 2::-1], 0.0,
                                             f32(sh_hi[j][64:128, :, 0:L - 1]), ALU.max, ALU.subtract)\
                        .then_inc(a_lo[j], 1)

            dve.wait_ge(s_prepg, PREP_GA)
            with dve.Fori(0, PAIRS // CHAINS) as i:
                for j in range(CHAINS):
                    dve.wait_ge(a_rnd, i * CHAINS + j + 1)
                    if j == 0:
                        dve.wait_ge(a_c, i * CHAINS + 1)
                    dve.scalar_tensor_tensor(x_st[j][0:2 * XROWS, :], f32(x_rnd[j % 2][:, :]),
                                             c_sb[0:2 * XROWS, C_MX:C_MX + 1], x_raw[j][:, :],
                                             ALU.mult, ALU.add).then_inc(a_x, 1)
                for k in range(STEPS):
                    for j in range(CHAINS):
                        evac(j, k, i)
                for j in range(1, CHAINS, 2):
                    dve.wait_ge(a_c, i * CHAINS + j + 2)
                    dve.tensor_scalar(miu[j][:, :], bank[4 + j][:, 0:C], 0.0, None, ALU.max).then_inc(a_miu1, 1)
                for j in range(1, CHAINS, 2):
                    dve.wait_ge(a_t, i * CHAINS + j + 1)
                    dve.tensor_copy(h_all[:, ds(i * CHAINS * CH + j * CH, CH), :],
                                    bank[j][0:T, :].rearrange("p (c d) -> p c d", c=CH)[:, :, 0:D]).then_inc(a_h, 1)

            def norm(p, s_ln):
                norm_stats(p, s_ln)
                norm_aggr(p, s_ln)

            def norm_stats(p, s_ln):
                for c in range(CH):
                    last = dve.bn_stats(stats[:, c, :], h_all[:, ds(p * CH + c, 1), :])
                last.then_inc(s_ln, 1)

            def norm_aggr(p, s_ln):
                dve.wait_ge(s_ln, 2 * p + 1)
                dve.memset(spare[:, :], 0.0)
                for c in range(CH):
                    last = dve.bn_aggr(aggr[:, c, :], stats[:, c, :])
                last.then_inc(s_ln, 1)

            def norm2(p, s_ln, s_inv, invs, row, s_out, dst, at):
                dve.wait_ge(s_ln, 2 * p + 2)
                dve.wait_ge(s_inv, invs * (p + 1))
                for c in range(CH):
                    last = dve.tensor_scalar(dst[:, at(c), :], h_all[:, ds(p * CH + c, 1), :],
                                             aggr[:, c, 0:1], inv[:, row, c:c + 1], ALU.subtract, ALU.mult)
                last.then_inc(s_out, 1)

            def norm2_b(p):
                wait(dve, b_xn, p)
                norm2(p, b_ln, b_inv, 7, 6, b_z, z, lambda c: slice(c, c + 1))

            def residual(p, b):
                dve.wait_ge(b_f, 2 * p + b + 1)
                rows = h_all[:, ds(p * CH + 2 * b, 2), :]
                for k in range(2):
                    part = bank[0][0:T, 0:256].rearrange("p (c a d) -> p c a d", c=2, a=2)[:, :, k, :]
                    if k == 0:
                        dve.tensor_tensor(z2[:, :, :], part, rows, ALU.add).then_inc(b_half, 1)
                        dve.wait_ge(b_half, 2 * p + b + 1)
                    else:
                        dve.tensor_tensor(rows, part, z2[:, :, :], ALU.add).then_inc(b_res, 1)

            def step_b(p, j, old2, old, new, ln):
                def caps(v, c):
                    n = 2 * v + c
                    dve.wait_ge(b_exp, 16 * (p - 1) + n + 1)
                    for hh in range(2):
                        h = (2 * v + hh) % H
                        part = prob[n % 4][:, hh, :]
                        last = dve.tensor_scalar(part, part, cap_hi[0:T, h:h + 1], cap_lo[0:T, h:h + 1],
                                                 ALU.min, ALU.max)
                    last.then_inc(b_cap, 1)

                def unit(k):
                    c, q = k // 3, k % 3
                    if k >= 12:
                        h = k - 12
                        dve.wait_ge(b_ev, 20 * p + k + 1)
                        dve.tensor_tensor(m2[j][0:64, h, :], bank[2 + h % 2][0:64, 0:C], f32(m1[j][0:64, h, :]),
                                          ALU.subtract).then_inc(b_gl, 1)
                    elif q < 2:
                        if k == 0:
                            wait(dve, b_qkw, 2 * p)
                        dve.wait_ge(b_ev, 20 * p + k + 1)
                        dve.tensor_reduce(qk[:, c, q, :], sq[q][:, :].rearrange("p (h d) -> p h d", h=H),
                                          AX.X, ALU.add).then_inc(b_red, 1)

                if isinstance(p, int) and p == 0:
                    dve.wait_ge(a_h, PAIRS + 1)
                    norm(0, b_ln)
                    norm2_b(0)
                for v in range(8):
                    if new and v == 0:
                        dve.wait_ge(b_rnd, 2 * p + 2)
                        wait(dve, b_sc, 16 * (p - 1))
                        dve.scalar_tensor_tensor(s1[j][:, :], f32(rnd1[:, :]), c_sb[:, C_MS1:C_MS1 + 1],
                                                 bank[0][:, 0:C], ALU.mult, ALU.add).then_inc(b_s1, 1)
                    rest = list(units(v)) if new else []
                    for c in range(2):
                        if old:
                            caps(v, c)
                        if rest:
                            unit(rest.pop(0))
                    for k in rest:
                        unit(k)
                    if v == 1 and old2:
                        residual(p - 2, 1)
                    if v == 7 and old:
                        residual(p - 1, 0)
                    if new and v == 5:
                        dve.wait_ge(b_rnd2, p + 1)
                        dve.scalar_tensor_tensor(s2[j][64:S_ROWS, :], f32(rnd2[64:S_ROWS, :]),
                                                 c_sb[64:S_ROWS, C_MS2:C_MS2 + 1], bank[0][64:S_ROWS, 0:C],
                                                 ALU.mult, ALU.add).then_inc(b_s2, 1)
                    if ln and v == 0:
                        norm_stats(p + 1, b_ln)
                    if ln and v == 1:
                        norm_aggr(p + 1, b_ln)
                    if ln and v == 3:
                        norm2_b(p + 1)

            def step_b_tail(p, j, old2, old, new, ln):
                if isinstance(p, int) and p == PAIRS + 1:
                    residual(p - 2, 1)
                else:
                    step_b(p, j, old2, old, new, ln)

            steps(dve, step_b_tail, BODY_B)

            def norm2_c(p):
                norm2(p, c_ln, c_inv, 2, 1, c_hn, hn_all, lambda c: ds(p * CH + c, 1))

            def gate_step(p, n):
                def done(ins):
                    ins.then_inc(c_gate, 1)

                def wide(t):
                    return t.unsqueeze(2).to_broadcast([T, CH, E])

                dsc = desc[:, :].unsqueeze(1).to_broadcast([T, CH, E])
                if n == 0:
                    dve.wait_ge(c_lg, p + 1)
                else:
                    dve.wait_ge(c_gate, GATE * p + (n - 1 if n == GATE_D else n))
                if n == 0:
                    done(dve.tensor_tensor(lg[:, 0, :, :],
                                           bank[1][0:T, 0:CH * W_ROWS].rearrange("p (c e) -> p c e", c=CH)[:, :, 0:E],
                                           gb_sb[:, :].unsqueeze(1).to_broadcast([T, CH, E]), ALU.add))
                k, src = (0, lg[:, 0, :, :]) if n < 7 else (1, lg[:, 3, :, :])
                if n in (1, 7):
                    done(dve.tensor_reduce(top[:, 2 * k, :], src, AX.X, ALU.max))
                if n in (2, 9):
                    done(dve.tensor_tensor(lg[:, 1, :, :], src, wide(top[:, 2 * k, :]), ALU.is_equal))
                if n in (3, 10):
                    done(dve.tensor_tensor(lg[:, 5, :, :], lg[:, 1, :, :], dsc, ALU.mult))
                if n in (4, 11):
                    done(dve.tensor_reduce(top[:, 2 * k + 1, :], lg[:, 5, :, :], AX.X, ALU.max))
                if n in (5, 12):
                    done(dve.tensor_tensor(lg[:, 2 + 2 * k, :, :], lg[:, 5, :, :], wide(top[:, 2 * k + 1, :]),
                                           ALU.is_equal))
                if n == 6:
                    done(dve.scalar_tensor_tensor(lg[:, 3, :, :], lg[:, 2, :, :], -BIG, lg[:, 0, :, :],
                                                  ALU.mult, ALU.add))
                if n == 8:
                    done(dve.tensor_tensor(top[:, 6, :], top[:, 2, :], top[:, 0, :], ALU.subtract))
                if n == 13:
                    dve.wait_ge(c_e, p + 1)
                    done(dve.tensor_scalar(top[:, 8, :], top[:, 7, :], 1.0, None, ALU.add))
                if n == 14:
                    done(dve.reciprocal(top[:, 9, :], top[:, 8, :]))
                if n == 15:
                    done(dve.tensor_tensor(top[:, 10, :], top[:, 9, :], top[:, 7, :], ALU.mult))
                if n == 16:
                    dve.tensor_tensor(lg[:, 5, :, :], lg[:, 2, :, :], wide(top[:, 9, :]), ALU.mult)
                    done(dve.tensor_tensor(lg[:, 6, :, :], lg[:, 4, :, :], wide(top[:, 10, :]), ALU.mult))
                if n == 17:
                    wait(dve, c_wtt, p)
                    dve.tensor_tensor(wtok[:, :, 0:E], lg[:, 5, :, :], lg[:, 6, :, :], ALU.add)
                    done(dve.tensor_tensor(wtok[:, :, 32:32 + E], lg[:, 5, :, :], lg[:, 6, :, :], ALU.add))

            def result(p, n):
                sums = bank[1][0:T, :].rearrange("p (c a d) -> p c a d", c=CH, a=2)
                if n == 0:
                    dve.wait_ge(c_f, p + 1)
                    dve.tensor_tensor(yt2[:, :, :], sums[:, :, 0, :], hn_all[:, ds(p * CH, CH), :], ALU.add)\
                        .then_inc(c_half, 1)
                if n == 1:
                    dve.wait_ge(c_half, p + 1)
                    dve.tensor_tensor(yt[:, :, :], sums[:, :, 1, :], yt2[:, :, :], ALU.add).then_inc(c_fin, 1)
                if n == 2:
                    dve.wait_ge(c_fin, 4 * p + 1)
                    for c in range(CH):
                        last = dve.bn_stats(stats2[:, c, :], yt[:, c, :])
                    last.then_inc(c_fin, 1)
                if n == 3:
                    dve.wait_ge(c_fin, 4 * p + 2)
                    dve.memset(spare[:, :], 0.0)
                    for c in range(CH):
                        last = dve.bn_aggr(aggr2[:, c, :], stats2[:, c, :])
                    last.then_inc(c_fin, 1)
                if n == 4:
                    dve.wait_ge(c_fin, 4 * p + 3)
                    dve.wait_ge(c_pinv, 2 * p + 2)
                    wait(dve, c_gres, 2 * p)
                    for c in range(CH):
                        last = dve.tensor_scalar(yz[:, 0, c, :], yt[:, c, :], aggr2[:, c, 0:1], inv2[:, 1, c:c + 1],
                                                 ALU.subtract, ALU.mult)
                    last.then_inc(c_fin, 1)

            def stack_c(p, j):
                dve.wait_ge(c_rnd, p + 1)
                wait(dve, c_up, 16 * (p - 1))
                dve.scalar_tensor_tensor(s1[j][:, :], f32(rnd1[:, :]), c_sb[:, C_MS1:C_MS1 + 1],
                                         bank[7][:, 0:C], ALU.mult, ALU.add).then_inc(c_s1, 1)

            GATE_AT = {2: (0, 1), 3: (2, 3), 4: (4, 5), 5: (6, 7), 6: (8, 9), 7: (10, 11), 8: (12,),
                       9: (13, 14), 10: (15, 16), 11: (17,)}
            RESULT_AT = {5: 0, 6: 1, 8: 2, 9: 3, 12: 4}

            def step_c(p, j, old2, old, new, ln):
                def gate(g):
                    dve.wait_ge(c_relu, 16 * (p - 1) + g + 1)
                    if g == 0:
                        dve.wait_ge(c_wbs, p)
                    wait(dve, c_dn, 8 * (p - 1) + g // 2 - 3)
                    dve.tensor_tensor(gated[g % 8][:, :], relu_sb[g % 4][:, :], wb[1 - j][:, :], ALU.mult)\
                        .then_inc(c_gated, 1)

                for g in range(16):
                    if old:
                        gate(g)
                    if ln and g == 0:
                        norm_stats(p + 1, c_ln)
                    if ln and g == 1:
                        norm_aggr(p + 1, c_ln)
                    at = GATE_AT.get(g, ()) if new else ()
                    for n in at[:1]:
                        gate_step(p, n)
                    if ln and g == 7:
                        norm2_c(p + 1)
                    if old2 and g in RESULT_AT:
                        result(p - 2, RESULT_AT[g])
                    for n in at[1:]:
                        gate_step(p, n)
                    if new and g == 13:
                        dve.wait_ge(c_rndw, p + 1)
                        wait(dve, c_dn, 8 * (p - 1))
                        dve.scalar_tensor_tensor(wt[j][:, :], f32(rnd2[0:48, :]), c_sb[0:48, C_MG:C_MG + 1],
                                                 bank[0][0:48, 0:C], ALU.mult, ALU.add).then_inc(c_wt, 1)
                    if ln and g == 14:
                        stack_c(p + 1, 1 - j)

            dve.wait_ge(b_res, 2 * PAIRS)
            norm(0, c_ln)
            norm2_c(0)
            stack_c(0, 0)
            steps(dve, step_c, BODY_C)

        @block.tensor
        def _(pe):
            pe.wait_ge(ld_a, 16 * len(A_LOADS))
            for h in range(H):
                pe.matmul(bank[6][:, h * D:(h + 1) * D], wqT_sb[:, h, :], wkT_sb[:, h, :], start=True, stop=True)
                last = pe.matmul(bank[7][:, h * D:(h + 1) * D], wvT_sb[:, h, :], woT_sb[:, h, :],
                                 start=True, stop=True)
            last.then_inc(s_wprod, 1)
            pe.wait_ge(s_prep, PREP_W)
            pe.wait_ge(s_prepg, PREP_GA)

            def three(dst, w, hi, lo):
                dst = dst[:, 0:C].rearrange("p (b l) -> p b l", b=2)
                pe.matmul(dst, w24_hi[:, w, :], hi, start=False, stop=False)
                pe.matmul(dst, w24_lo[:, w, :], hi, start=False, stop=False)
                return pe.matmul(dst, w24_hi[:, w, :], lo, start=False, stop=True)

            with pe.Fori(0, PAIRS // CHAINS) as i:
                for k in range(STEPS):
                    for j in range(CHAINS):
                        if k == 0:
                            pe.wait_ge(a_x, i * CHAINS + j + 1)
                            pe.wait_ge(a_h, i * CHAINS + 1)
                        else:
                            pe.wait_ge(a_lo[j], (i * STEPS + k) * 2)
                        last = pe.matmul(bank[j][:, 0:C], aw[:, :], x_st[j][:, :], start=True, stop=k == 0)
                        if k:
                            last = three(bank[j], 0, st_hi[j][:, :, 0:L], st_lo[j][:, :, 0:L])
                        last.then_inc(a_mm[j], 1)
                for j in range(CHAINS):
                    pe.wait_ge(a_lo[j], (i * STEPS + STEPS) * 2)
                    pe.matmul(bank[4 + j][:, 0:C], cw[:, :], x_st[j][:, :], start=True, stop=False)
                    three(bank[4 + j], 1, sh_hi[j][:, :, :], sh_lo[j][:, :, :]).then_inc(a_c, 1)
                for j in range(CHAINS):
                    pe.wait_ge((a_miu0, a_miu1)[j % 2], i * 2 + j // 2 + 1)
                    for c in range(CH):
                        last = pe.transpose(bank[j][0:T, c * 128:(c + 1) * 128], miu[j][:, c * T:(c + 1) * T], ident)
                    last.then_inc(a_t, 1)

            def products(p, v, jj, hh):
                b = v // 4
                if hh == 0:
                    pe.wait_ge(b_cap, 16 * p + 2 * v + 2)
                    if v % 4 == 0:
                        wait(pe, b_y, 2 * p + b)
                h = (2 * v + hh) % H
                for c in range(2):
                    last = pe.matmul(bank[1][64 * c:64 * c + 64, 0:L], u_sb[jj][:, 2 * b + c, h * D:(h + 1) * D],
                                     prob[(2 * v + c) % 4][:, hh, :], start=h == 0, stop=h == H - 1)
                if hh == 1:
                    last.then_inc(b_pv, 1)

            def fold_b(p, b):
                pe.wait_ge(b_y, 2 * p + b + 1)
                for c in range(2):
                    last = pe.transpose(bank[0][0:T, c * 128:(c + 1) * 128], y_att[:, c * T:(c + 1) * T], ident)
                last.then_inc(b_f, 1)

            def step_b(p, j, old2, old, new, ln):
                o = 1 - j

                def scores(v, c):
                    b, hp, n = v // 4, v % 4, 2 * v + c
                    wait(pe, b_exp, 16 * (p - 1) + n - 3)
                    cols = slice((2 * b + c) * T, (2 * b + c + 1) * T)
                    ps = bank[4 + n % 4][0:T, 0:C].rearrange("p (h l) -> p h l", h=2)
                    pe.matmul(ps, s1[o][:, cols], m1[o][:, 2 * hp:2 * hp + 2, b * L:(b + 1) * L],
                              start=True, stop=False)
                    pe.matmul(ps, s2[o][:, cols], m2[o][:, 2 * hp:2 * hp + 2, b * L:(b + 1) * L],
                              start=False, stop=True).then_inc(b_sc, 1)

                def unit(k):
                    c, q, dst = k // 3, k % 3, bank[2 + k % 2]
                    if k < 2:
                        wait(pe, b_gl, 8 * (p - 1) + 7 + k)
                    elif k < 14:
                        pe.wait_ge(b_ev, 20 * p + k - 1)
                    else:
                        pe.wait_ge(b_gl, 8 * p + k - 13)
                    if k == 0:
                        pe.wait_ge(b_s1, p + 1)
                    for hi_lo, first in ((0, True), (1, False)):
                        if k < 12:
                            w = (wqku_hi, wqku_lo)[hi_lo]
                            last = pe.matmul(dst[0:T, :], s1[j][:, c * T:(c + 1) * T], w[:, q, :],
                                             start=first, stop=not first)
                        else:
                            w = (wg_hi, wg_lo)[hi_lo]
                            last = pe.matmul(dst[:, 0:C], w[:, k - 12, :, :].rearrange("p a d -> p (a d)"),
                                             s1[j][:, :], start=first, stop=not first)
                    last.then_inc(b_pj, 1)

                for v in range(8):
                    if new and v == 0:
                        pe.wait_ge(b_xn, p + 1)
                        wait(pe, b_s2, p)
                        wait(pe, b_res, 2 * (p - 1) - 1)
                        for c in range(CH):
                            last = pe.transpose(bank[0][:, c * T:(c + 1) * T],
                                                xn[:, c, :, :].rearrange("p a d -> p (a d)"), ident[0:T, 0:T])
                        last.then_inc(b_xt, 1)
                    if old and v == 0:
                        pe.wait_ge(b_row, 32 * p)
                        pe.wait_ge(b_gl, 8 * p)
                    rest = list(units(v)) if new else []
                    for c in range(2):
                        if old:
                            scores(v, c)
                        if rest:
                            unit(rest.pop(0))
                    for hh in range(2):
                        if v == 0 and old2:
                            products(p - 2, 7, j, hh)
                        if v > 0 and old:
                            products(p - 1, v - 1, o, hh)
                        if rest:
                            unit(rest.pop(0))
                    if old2 and v == 1:
                        if new:
                            pe.wait_ge(b_s1, p + 1)
                        fold_b(p - 2, 1)
                    if new and v == 5:
                        pe.wait_ge(b_qkw, 2 * p + 2)
                        wait(pe, b_res, 2 * (p - 1))
                        for c in range(CH):
                            last = pe.transpose(bank[0][0:S_ROWS, c * T:(c + 1) * T], qkw[:, c, :], ident[0:T, 0:T])
                        last.then_inc(b_qt, 1)
                    if old and v == 7:
                        if new:
                            pe.wait_ge(b_s2, p + 1)
                        wait(pe, b_res, 2 * (p - 1))
                        fold_b(p - 1, 0)

            def step_b_tail(p, j, old2, old, new, ln):
                if isinstance(p, int) and p == PAIRS + 1:
                    products(p - 2, 7, j, 0)
                    products(p - 2, 7, j, 1)
                    wait(pe, b_res, 2 * (p - 1) - 1)
                    fold_b(p - 2, 1)
                else:
                    step_b(p, j, old2, old, new, ln)

            pe.wait_ge(s_prepg, PREP_G)
            pe.wait_ge(a_h, PAIRS + 1)
            steps(pe, step_b_tail, BODY_B)

            def down(p, v, jj):
                y = bank[6]
                if v == 0:
                    wait(pe, c_y, p)
                    pe.matmul(y[:, 0:C], b2_hi[:, :], wt[jj][:, :], start=True, stop=False, skip_group_check=True)
                    pe.matmul(y[:, 0:C], b2_lo[:, :], wt[jj][:, :], start=False, stop=False, skip_group_check=True)
                pe.wait_ge(c_gated, 16 * p + 2 * v + 2)
                for k in range(2):
                    g = 2 * v + k
                    last = pe.matmul(y[64 * k:64 * k + 64, 0:C], w2_sb[:, g, :], gated[g % 8][:, :],
                                     start=False, stop=v == 7, skip_group_check=True)
                last.then_inc(c_dn, 1)

            def tokens_c(p):
                pe.wait_ge(c_xn, p + 1)
                wait(pe, c_lgs, p)
                for c in range(CH):
                    last = pe.transpose(bank[7][:, c * T:(c + 1) * T],
                                        xn[:, c, :, :].rearrange("p a d -> p (a d)"), ident[0:T, 0:T])
                last.then_inc(c_xt, 1)

            def step_c(p, j, old2, old, new, ln):
                o = 1 - j

                def up(g):
                    wait(pe, c_relu, 16 * (p - 1) + g - 3)
                    for w, first in ((w1_hi, True), (w1_lo, False)):
                        last = pe.matmul(bank[2 + g % 4][:, 0:C], w[:, g, :], s1[o][:, :], start=first, stop=not first)
                    last.then_inc(c_up, 1)

                for v in range(8):
                    if old:
                        up(2 * v)
                        up(2 * v + 1)
                    if old and v == 0:
                        pe.wait_ge(c_wt, p)
                        pe.matmul(bank[0][:, 0:C], sel[:, :], wt[o][:, :], start=True, stop=True).then_inc(c_wb, 1)
                    if new and v == 7:
                        pe.wait_ge(c_gate, GATE * (p + 1))
                        wait(pe, c_wbs, p)
                        for c in range(CH):
                            last = pe.transpose(bank[0][0:W_ROWS, c * T:(c + 1) * T], wtok[:, c, :], ident[0:T, 0:T])
                        last.then_inc(c_wtt, 1)
                    if v < 2 and old2:
                        down(p - 2, v + 6, j)
                    if v >= 2 and old:
                        down(p - 1, v - 2, o)
                    if new and v == 0:
                        pe.wait_ge(c_s1, p + 1)
                        for w, first in ((gw_hi, True), (gw_lo, False)):
                            last = pe.matmul(bank[7][0:W_ROWS, 0:C], w[:, :], s1[j][:, :], start=first, stop=not first)
                        last.then_inc(c_lgt, 1)
                    if new and v == 1:
                        pe.wait_ge(c_lgs, p + 1)
                        wait(pe, c_fin, 4 * (p - 3) + 1)
                        for c in range(CH):
                            last = pe.transpose(bank[1][0:T, c * W_ROWS:(c + 1) * W_ROWS], lgt[:, c * T:(c + 1) * T],
                                                ident[0:W_ROWS, 0:W_ROWS])
                        last.then_inc(c_lg, 1)
                    if old2 and v == 3:
                        pe.wait_ge(c_y, p - 1)
                        if new:
                            pe.wait_ge(c_gate, GATE * p + 1)
                        for c in range(CH):
                            last = pe.transpose(bank[1][0:T, c * 128:(c + 1) * 128], y_moe[:, c * T:(c + 1) * T], ident)
                        last.then_inc(c_f, 1)
                    if ln and v == 6:
                        tokens_c(p + 1)

            pe.wait_ge(b_res, 2 * PAIRS)
            tokens_c(0)
            steps(pe, step_c, BODY_C)


PREP_A = 6
PREP_W = 9
PREP_GA = 5 * CHAINS
PREP_G = PREP_GA + 28
GATE_D = 9
GATE = 18


def kernel(**inputs):
    import concourse.bacc as bacc
    from concourse.bass_utils import run_bass_kernel_spmd

    def a(name):
        return np.asarray(inputs[name])

    def rows(x, n):
        return np.broadcast_to(x[None], (n,) + x.shape)

    def stacked(w, rev_left, rev_right, fwd_left, fwd_right, bias):
        o = np.zeros((AROWS, 128), np.float32)
        for g in range(4):
            f = slice(g * D_IN, (g + 1) * D_IN)
            r = slice(XROWS + g * D_IN, XROWS + (g + 1) * D_IN)
            for half, fwd, rev in ((0, fwd_left, rev_left), (1, fwd_right, rev_right)):
                cols = slice(half * D, half * D + D)
                if fwd:
                    o[f, cols] = w.T
                if rev:
                    o[r, cols] = w.T
        o[AROWS - 2:, :] = np.concatenate([bias, bias])
        return o

    def bias_rows(b):
        o = np.zeros((AROWS, 128), np.float32)
        o[AROWS - 2:, :] = np.concatenate([b, b])
        return o

    x = a("x").reshape(PAIRS, 2, D_IN, L).transpose(0, 2, 1, 3)
    xr = np.concatenate([np.tile(x, (1, 4, 1, 1)), np.tile(x[..., ::-1], (1, 4, 1, 1))], axis=1)
    W2T, W4T = a("L0_tok_W2").T, a("L0_tok_W4").T
    w2bd = np.zeros((128, 128), np.float32)
    w2bd[:D, :D] = W2T
    w2bd[D:, D:] = W2T
    w_q, w_k, w_v = a("L0_attn_W_q"), a("L0_attn_W_k"), a("L0_attn_W_v")
    qT, kT, vT = (w.transpose(2, 0, 1) for w in (w_q, w_k, w_v))
    oT = a("L0_attn_W_o").reshape(D, H, D).transpose(2, 1, 0)
    b2 = np.zeros((48, 128), np.float32)
    b2[0:E, 0:D] = b2[32:32 + E, 0:D] = a("L0_ffn_b2")
    gate_w = np.zeros((128, W_ROWS), np.float32)
    gate_w[:, 0:E] = np.tile(a("L0_ffn_gate_w"), (2, 1))
    w1 = a("L0_ffn_w1").reshape(E, D, G, R)
    arrays = {
        "cst": constants(),
        "xr": xr.reshape(PAIRS, 2 * XROWS, C),
        "aw1": stacked(a("L0_tok_W1"), False, True, True, False, a("L0_tok_b1")),
        "aw2": bias_rows(a("L0_tok_b2")),
        "cw1": stacked(a("L0_tok_W3"), False, False, True, True, a("L0_tok_b3")),
        "cw2": bias_rows(a("L0_tok_b4")),
        "w24": np.stack([w2bd, np.tile(W4T, (2, 2))], axis=1),
        "wqT": np.concatenate([qT, qT], axis=2),
        "wkT": kT,
        "wvT": np.concatenate([vT, vT], axis=2),
        "woT": oT,
        "wq": np.tile(w_q.transpose(1, 0, 2).reshape(D, H * D), (2, 1)),
        "wk": np.tile(w_k.transpose(1, 0, 2).reshape(D, H * D), (2, 1)),
        "gam": rows(a("L0_attn_gamma").reshape(H), 128),
        "lns": rows(a("L0_attn_ln_scale"), T),
        "gw": gate_w,
        "gb": rows(a("L0_ffn_gate_b"), T),
        "w1": np.tile(w1.transpose(1, 2, 0, 3).reshape(D, G, 128), (2, 1, 1)),
        "b1": a("L0_ffn_b1").reshape(E, G, R).transpose(0, 2, 1).reshape(128, G),
        "w2": a("L0_ffn_w2").reshape(E, G, R, D).transpose(0, 2, 1, 3).reshape(128, G, D),
        "b2": b2,
        "fg": rows(a("L0_ffn_gamma"), T),
        "fb": rows(a("L0_ffn_beta"), T),
    }
    nc = bacc.Bacc("TRN2", target_bir_lowering=False, num_devices=1)
    ins, args = {}, {}
    for name, v in arrays.items():
        v = np.ascontiguousarray(v)
        ins[f"in_{name}"] = v
        args[name] = nc.dram_tensor(f"in_{name}", v.shape, mybir.dt.from_np(v.dtype), kind="ExternalInput").ap()
    out = nc.dram_tensor("out", (B, L, D), F32, kind="ExternalOutput").ap()
    build(nc, **args, out=out)
    r = run_bass_kernel_spmd(nc, [ins], core_ids=[0])
    return r.results[0]["out"]
```

```python
from contextlib import ExitStack

import numpy as np

import concourse.bass as bass
from concourse import mybir

ALU = mybir.AluOpType
ACT = mybir.ActivationFunctionType
AX = mybir.AxisListType
F32 = mybir.dt.float32
F32R = mybir.dt.float32r
ds = bass.ds

B, D_IN, L = 32, 4, 250
D = 64
H = 8
E = 16
F = 128
G = 16
R = 128 // E
STEPS = 8
T = L // 2
PAIRS = B // 2
C = 2 * L
CH = 4
NCHUNK = PAIRS * CH
CHAINS = 4
EPS = 1e-5
BIG = 3.0e38

XROWS = 4 * D_IN
AROWS = 2 * XROWS + 2
Q_ROW, ONE_ROW, K_ROW, S_ROWS = 64, 80, 96, 112

GW_LO = 32
W_ROWS = 96

C_IDENT, C_SEL = 0, 128
C_MX, C_MW, C_MS1, C_MS2, C_MG = 256, 257, 258, 259, 260
C_IND = 261
C_COLS = C_IND + H


def constants():
    c = np.zeros((128, C_COLS), np.float32)
    c[:, C_IDENT:C_IDENT + 128] = np.eye(128)
    for half in range(2):
        for g in range(4):
            rows = slice(half * XROWS + g * D_IN, half * XROWS + (g + 1) * D_IN)
            c[rows, C_MX] = -1.0 if g >= 2 else 0.0
            c[rows, C_MW] = -1.0 if g % 2 else 0.0
    c[AROWS - 1, C_MW] = -1.0
    c[64:, C_MS1] = -1.0
    c[Q_ROW + H:Q_ROW + 2 * H, C_MS2] = -1.0
    c[K_ROW + H:K_ROW + 2 * H, C_MS2] = -1.0
    for a in (1, 3):
        c[a * E:(a + 1) * E, C_MG] = -1.0
    for h in range(H):
        c[K_ROW + h, C_IND + h] = 1.0
        c[K_ROW + H + h, C_IND + h] = 1.0
    for e in range(E):
        c[e, C_SEL + e * R:C_SEL + (e + 1) * R] = 1.0
        c[E + e, C_SEL + e * R:C_SEL + (e + 1) * R] = 1.0
    return c


def build(nc, cst, xr, aw1, aw2, cw1, cw2, w24, wqT, wkT, wvT, woT, wq, wk, gam, lns,
          gw, gb, w1, b1, w2, b2, fg, fb, out):
    with ExitStack() as ctx:
        def sb(name, shape, dt=F32):
            return ctx.enter_context(nc.sbuf_tensor(name, shape, dt))

        def sem(name):
            return ctx.enter_context(nc.semaphore(name))

        def f32(ap):
            return ap.bitcast(F32)

        bank = [ctx.enter_context(nc.psum_tensor(f"bank{i}", [128, 512], F32)) for i in range(8)]

        c_sb = sb("c_sb", [128, C_COLS])
        ident = c_sb[:, C_IDENT:C_IDENT + 128]
        aw1_sb, aw2_sb = sb("aw1_sb", [AROWS, 128]), sb("aw2_sb", [AROWS, 128])
        cw1_sb, cw2_sb = sb("cw1_sb", [AROWS, 128]), sb("cw2_sb", [AROWS, 128])
        w24_sb = sb("w24_sb", [128, 2, 128])
        gam_sb, lns_sb = sb("gam_sb", [128, H]), sb("lns_sb", [T, D])
        gwraw, gb_sb = sb("gwraw", [128, W_ROWS]), sb("gb_sb", [T, E])
        b1_sb, w2_sb = sb("b1_sb", [128, G]), sb("w2_sb", [128, G, D])
        b2raw = sb("b2raw", [4 * E, 128])
        fg_sb, fb_sb = sb("fg_sb", [T, D]), sb("fb_sb", [T, D])

        aw, cw = sb("aw", [AROWS, 128], F32R), sb("cw", [AROWS, 128], F32R)
        w24_hi, w24_lo = sb("w24_hi", [128, 2, 128], F32R), sb("w24_lo", [128, 2, 128], F32R)
        wqku_hi = sb("wqku_hi", [128, 3, H * D], F32R)
        wqku_lo = sb("wqku_lo", [128, 3, H * D], F32R)
        wg_hi, wg_lo = sb("wg_hi", [128, H * D], F32R), sb("wg_lo", [128, H * D], F32R)
        gw_st = sb("gw_st", [128, W_ROWS], F32R)
        w1_hi, w1_lo = sb("w1_hi", [128, G, 128], F32R), sb("w1_lo", [128, G, 128], F32R)
        b2_st = sb("b2_st", [4 * E, 128], F32R)
        sel = sb("sel", [2 * E, 128], F32R)
        g2 = sb("g2", [128, H])
        gneg = sb("gneg", [128, H])
        cap_lo, cap_hi = sb("cap_lo", [128, H]), sb("cap_hi", [128, H])
        spare, spare2 = sb("spare", [T, 1]), sb("spare2", [T, 1])
        mhalf, eps = sb("mhalf", [T, CH]), sb("eps", [T, CH])

        h_all = sb("h_all", [T, NCHUNK, D])

        stats, aggr = sb("stats", [T, CH, 6]), sb("aggr", [T, CH, 2])
        inv = sb("inv", [T, 8, CH])
        hc, z, z2 = sb("hc", [T, CH, D]), sb("z", [T, CH, D]), sb("z2", [T, CH, D])
        xn = sb("xn", [T, CH, 2, D])
        rnd1, rnd2 = sb("rnd1", [128, C], F32R), sb("rnd2", [128, C], F32R)
        s1 = [sb(f"s1_{j}", [128, C], F32R) for j in range(2)]
        m2 = [sb(f"m2_{j}", [S_ROWS, H, C], F32R) for j in range(2)]
        qk = sb("qk", [T, CH, 2, H])
        qkw = sb("qkw", [T, CH, S_ROWS])

        lg = sb("lg", [T, 8, CH, E])
        top = sb("top", [T, 12, CH])
        desc = sb("desc", [T, E])
        wtok = sb("wtok", [T, CH, W_ROWS])

        def phase(*tensors):
            with ExitStack() as scope:
                return [[scope.enter_context(nc.sbuf_tensor(f"{name}{j}", shape, dt)) for j in range(n)]
                        for name, n, shape, dt in tensors]

        x_st, st_hi, st_lo, sh_hi, sh_lo, miu, x_raw, x_rnd, (wqv_sb,), (wko_sb,), (wraw,), (w1raw,), (awt,), (awr,) = phase(
            ("x_st", CHAINS, [AROWS, C], F32R),
            ("st_hi", CHAINS, [128, 2, L + 1], F32R), ("st_lo", CHAINS, [128, 2, L + 1], F32R),
            ("sh_hi", CHAINS, [128, 2, L], F32R), ("sh_lo", CHAINS, [128, 2, L], F32R), ("miu", CHAINS, [128, C], F32),
            ("x_raw", CHAINS, [2 * XROWS, C], F32), ("x_rnd", CHAINS, [2 * XROWS, C], F32R),
            ("wqv_sb", 1, [128, H, 128], F32), ("wko_sb", 1, [128, H, 64], F32),
            ("wraw", 1, [128, 4, H * D], F32), ("w1raw", 1, [128, G, 128], F32),
            ("awt", 1, [AROWS, 2, 128], F32), ("awr", 1, [AROWS, 2, 128], F32R))
        hn_all = sb("hn_all", [T, NCHUNK, D])
        lgt = sb("lgt", [W_ROWS, C])
        wt = [sb(f"wt{j}", [4 * E, C], F32R) for j in range(2)]
        m1, s2, u_sb, sq, sq2, prob, y_att = phase(
            ("m1_", 2, [128, H, C], F32R), ("s2_", 2, [S_ROWS, C], F32R), ("u", 2, [T, CH, H * D], F32), ("sq", 2, [T, H, D], F32),
            ("sq2_", 2, [T, H, D // 2], F32),
            ("prob", 4, [T, 2, L], F32), ("y_att", 2, [128, L], F32))
        relu_sb, gated, (y_moe,), (yt,), (yt2,), (stats2,), (aggr2,), (inv2,), (yz,), (res,), wb = phase(
            ("relu", 4, [128, C], F32), ("gated", 8, [128, C], F32), ("y_moe", 1, [128, C], F32),
            ("yt", 1, [T, CH, D], F32), ("yt2_", 1, [T, CH, D], F32), ("stats2_", 1, [T, CH, 6], F32), ("aggr2_", 1, [T, CH, 2], F32),
            ("inv2_", 1, [T, 4, CH], F32), ("yz", 1, [T, 4, CH, D], F32), ("res", 1, [T, CH, D], F32),
            ("wb", 2, [128, C], F32))

        ld_w, ld_a, ld_b = sem("ld_w"), sem("ld_a"), sem("ld_b")
        s_prep = sem("s_prep")
        s_prepg = sem("s_prepg")
        s_wprod = sem("s_wprod")
        a_xin = [sem(f"a_xin{j}") for j in range(CHAINS)]
        a_rnd, a_x = sem("a_rnd"), sem("a_x")
        a_mm = [sem(f"a_mm{j}") for j in range(CHAINS)]
        a_hi = [sem(f"a_hi{j}") for j in range(CHAINS)]
        a_lo = [sem(f"a_lo{j}") for j in range(CHAINS)]
        a_c, a_miu0, a_miu1, a_t, a_h = (sem(n) for n in ("a_c", "a_miu0", "a_miu1", "a_t", "a_h"))
        b_ln, b_inv, b_hc, b_z, b_xn, b_sum = (sem(n) for n in ("b_ln", "b_inv", "b_hc", "b_z", "b_xn", "b_sum"))
        b_xt, b_rnd, b_s1 = sem("b_xt"), sem("b_rnd"), sem("b_s1")
        b_pj, b_ev, b_red, b_gl = (sem(n) for n in ("b_pj", "b_ev", "b_red", "b_gl"))
        b_dup = [sem(f"b_dup{u}") for u in range(4)]
        b_qkw, b_qt, b_rnd2, b_s2, b_row = (sem(n) for n in ("b_qkw", "b_qt", "b_rnd2", "b_s2", "b_row"))
        b_sc, b_exp, b_cap, b_pv = sem("b_sc"), sem("b_exp"), sem("b_cap"), sem("b_pv")
        b_y, b_f, b_half, b_res = sem("b_y"), sem("b_f"), sem("b_half"), sem("b_res")
        c_ln, c_inv, c_hc, c_hn, c_xn = (sem(n) for n in ("c_ln", "c_inv", "c_hc", "c_hn", "c_xn"))
        c_xt, c_rnd, c_s1, c_lgt, c_lgs, c_lg = (sem(n) for n in ("c_xt", "c_rnd", "c_s1", "c_lgt", "c_lgs", "c_lg"))
        c_lsum, c_gate, c_e, c_wtt, c_rndw, c_wt = (sem(n) for n in ("c_lsum", "c_gate", "c_e", "c_wtt", "c_rndw", "c_wt"))
        c_up, c_wb, c_wbs, c_relu, c_gated, c_gatep, c_dn = (
            sem(n) for n in ("c_up", "c_wb", "c_wbs", "c_relu", "c_gated", "c_gatep", "c_dn"))
        c_y, c_f, c_half, c_fin, c_pinv, c_gres, c_pout, c_out = (
            sem(n) for n in ("c_y", "c_f", "c_half", "c_fin", "c_pinv", "c_gres", "c_pout", "c_out"))

        def full(t):
            return t[tuple(slice(None) for _ in t.shape)]

        def wait(eng, s, value):
            if not (isinstance(value, int) and value <= 0):
                eng.wait_ge(s, value)

        W_LOADS = [(wqv_sb[0:64, :, :], wqT), (wko_sb[0:64, :, :], wkT),
                   (wqv_sb[64:128, :, :], wvT), (wko_sb[64:128, :, :], woT)]
        A_LOADS = [(c_sb, cst), (aw1_sb, aw1), (aw2_sb, aw2), (cw1_sb, cw1), (cw2_sb, cw2),
                   (w24_sb, w24), (gam_sb, gam)]
        B_LOADS = [(wraw[:, 0, :], wq), (wraw[:, 1, :], wk), (lns_sb, lns), (gwraw, gw), (gb_sb, gb),
                   (w1raw, w1), (b1_sb, b1), (w2_sb, w2), (b2raw, b2), (fg_sb, fg), (fb_sb, fb)]

        BODY_B = (3, PAIRS - 1)
        BODY_C = (3, PAIRS - 1)

        def steps(eng, step, body):
            first, last = body
            for p in range(first):
                step(p, p % 2, p >= 2, p >= 1, True, True)
            with eng.Fori(0, (last - first) // 2) as i:
                for k in range(2):
                    step(i * 2 + (first + k), (first + k) % 2, True, True, True, True)
            for p in range(last, PAIRS + 2):
                step(p, p % 2, p - 2 < PAIRS, p - 1 < PAIRS, p < PAIRS, p + 1 < PAIRS)

        def first_step(p):
            return isinstance(p, int) and p == 0

        def is_g(k):
            return k >= 8 and k % 2 == 0

        def units(v):
            return range(0) if v == 0 else range(3 * (v - 1), 3 * v) if v < 3 else range(2 * v, 2 * v + 2)

        def wait_gated(eng, p, g):
            n_pool = sum(k <= g for k in POOL_GROUPS)
            if g in POOL_GROUPS:
                wait(eng, c_gatep, len(POOL_GROUPS) * p + n_pool)
            else:
                wait(eng, c_gated, (G - len(POOL_GROUPS)) * p + g + 1 - n_pool)

        def gate_group(eng, p, g, j, s_done):
            eng.wait_ge(c_relu, 16 * p + g + 1)
            if g in (0, POOL_GROUPS[0]):
                eng.wait_ge(c_wbs, p + 1)
            wait(eng, c_dn, 8 * p + g // 2 - 3)
            eng.tensor_tensor(gated[g % 8][:, :], relu_sb[g % 4][:, :], wb[j][:, :], ALU.mult).then_inc(s_done, 1)

        block = ctx.enter_context(nc.Block())

        @block.sync
        def _(sp):
            for dst, src in A_LOADS:
                sp.dma_start(full(dst), full(src)).then_inc(ld_a, 16)
            for j in range(CHAINS):
                sp.dma_start(x_raw[j][:, :], xr[j, :, :]).then_inc(a_xin[j], 16)
            for dst, src in B_LOADS:
                sp.dma_start(full(dst), full(src)).then_inc(ld_b, 16)

            with sp.Fori(1, PAIRS // CHAINS) as i:
                for j in range(CHAINS):
                    sp.wait_ge(a_x, i * CHAINS - (CHAINS - 1 - j))
                    sp.dma_start(x_raw[j][:, :], xr[ds(i * CHAINS + j, 1), :, :].rearrange("a r c -> (a r) c"))\
                        .then_inc(a_xin[j], 16)

            def duplicate(p, j, u):
                sp.wait_ge(b_ev, 16 * p + 9 + 2 * u)
                for a in range(2):
                    sp.dma_start(f32(m1[j][64 - 64 * a:128 - 64 * a, 2 * u + a, :]),
                                 f32(m1[j][64 * a:64 * a + 64, 2 * u + a, :])).then_inc(b_dup[u], 16)

            def step_b(p, j, old2, old, new, ln):
                if new:
                    duplicate(p, j, 0)
                    duplicate(p, j, 1)
                    sp.wait_ge(b_s2, p + 1)
                    wait(sp, b_sc, 16 * (p - 1))
                    for k in range(2):
                        sp.dma_start(f32(m2[j][ONE_ROW + k:ONE_ROW + k + 1, :, :]),
                                     f32(s2[j][Q_ROW + k * H:Q_ROW + (k + 1) * H, :])).then_inc(b_row, 16)
                    duplicate(p, j, 2)
                    duplicate(p, j, 3)

            steps(sp, step_b, BODY_B)

            with sp.Fori(0, PAIRS) as i:
                sp.wait_ge(c_pout, i + 1)
                sp.dma_start(out[ds(i * 2, 2), :, :].rearrange("b (k t) d -> t (b k) d", k=2), res[:, :, :])\
                    .then_inc(c_out, 16)
            sp.wait_ge(c_out, 16 * PAIRS)

        @block.gpsimd
        def _(gp):
            count = [0]

            def done(ins):
                count[0] += 1
                ins.then_inc(s_prepg, 1)
                gp.wait_ge(s_prepg, count[0])

            for j in range(CHAINS):
                for t in (st_hi[j], st_lo[j]):
                    done(gp.memset(f32(t[:, :, 0:1]), 0.0))
                for t in (sh_hi[j], sh_lo[j]):
                    done(gp.memset(f32(t[:, :, 0:1]), 0.0))
                    done(gp.memset(f32(t[:, :, L - 1:L]), 0.0))
                done(gp.memset(f32(x_st[j][32:34, :]), 1.0))
            for counter in (a_c, a_h):
                gp.memset(spare2[:, :], 0.0).then_inc(counter, 1)
                gp.wait_ge(counter, 1)
            for j in range(2):
                done(gp.memset(f32(m2[j][64:96, :, :]), 0.0))
            done(gp.memset(qkw[:, :, :], 0.0))
            done(gp.memset(wtok[:, :, :], 0.0))
            done(gp.memset(eps[:, :], EPS))
            done(gp.memset(mhalf[:, :], -0.5))
            done(gp.memset(qkw[:, :, ONE_ROW:ONE_ROW + 2], 1.0))
            done(gp.iota(lg[:, 7, 0, :].bitcast(mybir.dt.int32), [[-1, E]], base=E, channel_multiplier=0))
            done(gp.tensor_copy(desc[:, :], lg[:, 7, 0, :].bitcast(mybir.dt.int32)))

            gp.wait_ge(ld_a, 16 * len(A_LOADS))
            gp.wait_ge(ld_b, 16 * len(B_LOADS))
            for j in range(2):
                done(gp.tensor_copy(m2[j][K_ROW:S_ROWS, :, :],
                                    c_sb[K_ROW:S_ROWS, C_IND:C_IND + H].unsqueeze(2).to_broadcast([2 * H, H, C])))
            done(gp.tensor_copy(sel[:, :], c_sb[0:2 * E, C_SEL:C_SEL + 128]))
            gp.wait_ge(s_prep, PREP_W)
            for q, src in ((0, 0), (1, 1), (2, 3)):
                done(gp.tensor_copy(wqku_hi[:, q, :], wraw[:, src, :]))
            done(gp.tensor_copy(wg_hi[:, :], wraw[:, 2, :]))
            done(gp.tensor_copy(gw_st[:, :], gwraw[:, :]))
            done(gp.tensor_copy(b2_st[:, :], b2raw[:, :]))
            done(gp.tensor_copy(w1_hi[:, :, :], w1raw[:, :, :]))
            for q, src in ((0, 0), (1, 1), (2, 3)):
                done(gp.tensor_tensor(wqku_lo[:, q, :], wraw[:, src, :], f32(wqku_hi[:, q, :]), ALU.subtract))
            done(gp.tensor_tensor(wg_lo[:, :], wraw[:, 2, :], f32(wg_hi[:, :]), ALU.subtract))
            done(gp.tensor_tensor(gw_st[:, GW_LO:GW_LO + E], gwraw[:, GW_LO:GW_LO + E], f32(gw_st[:, GW_LO:GW_LO + E]),
                                  ALU.subtract))
            done(gp.tensor_tensor(b2_st[2 * E:4 * E, :], b2raw[2 * E:4 * E, :], f32(b2_st[2 * E:4 * E, :]),
                                  ALU.subtract))
            done(gp.tensor_tensor(w1_lo[:, :, :], w1raw[:, :, :], f32(w1_hi[:, :, :]), ALU.subtract))
            assert count[0] == PREP_G

            lns4 = lns_sb[:, :].unsqueeze(1).unsqueeze(1).to_broadcast([T, CH, 2, D])
            gneg4 = gneg[0:T, :].unsqueeze(1).unsqueeze(1).to_broadcast([T, CH, 2, H])

            def wide(t):
                return t.unsqueeze(2).to_broadcast([T, CH, D])

            def centred(p, s_out):
                gp.tensor_tensor(hc[:, :, :], h_all[:, ds(p * CH, CH), :], wide(aggr[:, :, 0]), ALU.subtract)\
                    .then_inc(s_out, 1)

            def b_scales(p):
                n = 7 * p
                gp.wait_ge(b_ln, 2 * p + 2)
                var = aggr[:, :, 1]
                gp.tensor_tensor(inv[:, 0, :], var, eps[:, :], ALU.add).then_inc(b_inv, 1)
                gp.wait_ge(b_inv, n + 1)
                gp.tensor_tensor(inv[:, 1, :], inv[:, 0, :], mhalf[:, :], ALU.pow).then_inc(b_inv, 1)
                gp.wait_ge(b_inv, n + 2)
                gp.tensor_tensor(inv[:, 2, :], var, inv[:, 1, :], ALU.mult).then_inc(b_inv, 1)
                gp.wait_ge(b_inv, n + 3)
                gp.tensor_tensor(inv[:, 3, :], inv[:, 2, :], inv[:, 1, :], ALU.mult).then_inc(b_inv, 1)
                gp.wait_ge(b_inv, n + 4)
                gp.tensor_tensor(inv[:, 4, :], inv[:, 3, :], eps[:, :], ALU.add).then_inc(b_inv, 1)
                gp.wait_ge(b_inv, n + 5)
                gp.tensor_tensor(inv[:, 5, :], inv[:, 4, :], mhalf[:, :], ALU.pow).then_inc(b_inv, 1)
                gp.wait_ge(b_inv, n + 6)
                gp.tensor_tensor(inv[:, 6, :], inv[:, 1, :], inv[:, 5, :], ALU.mult).then_inc(b_inv, 1)
                gp.wait_ge(b_inv, n + 7)
                centred(p, b_hc)
                gp.wait_ge(b_hc, p + 1)
                gp.tensor_tensor(z[:, :, :], hc[:, :, :], wide(inv[:, 6, :]), ALU.mult).then_inc(b_z, 1)
                gp.wait_ge(b_z, p + 1)
                wait(gp, b_xt, p)
                gp.tensor_tensor(xn[:, :, :, :], z[:, :, :].unsqueeze(2).to_broadcast([T, CH, 2, D]),
                                 lns4, ALU.mult).then_inc(b_xn, 1)

            def step_b(p, j, old2, old, new, ln):
                if first_step(p):
                    b_scales(0)
                if new:
                    for k in range(8):
                        q = k % 2
                        gp.wait_ge(b_ev, 16 * p + k + 1)
                        wait(gp, b_red, 8 * p + k - 1)
                        gp.tensor_tensor(sq2[q][:, :, :], sq[q][:, :, 0:D // 2], sq[q][:, :, D // 2:D], ALU.add)\
                            .then_inc(b_sum, 1)
                    gp.wait_ge(b_red, 8 * p + 8)
                    wait(gp, b_qt, p)
                    gp.tensor_tensor(
                        qkw[:, :, Q_ROW:Q_ROW + 2 * H].rearrange("p c (a h) -> p c a h", a=2),
                        qk[:, :, 0, :].unsqueeze(2).to_broadcast([T, CH, 2, H]), gneg4, ALU.mult).then_inc(b_qkw, 1)
                    gp.tensor_tensor(
                        qkw[:, :, K_ROW:K_ROW + 2 * H].rearrange("p c (a h) -> p c a h", a=2),
                        qk[:, :, 1, :].unsqueeze(2).to_broadcast([T, CH, 2, H]), gneg4, ALU.mult).then_inc(b_qkw, 1)
                if ln:
                    b_scales(p + 1)

            steps(gp, step_b, BODY_B)

            def c_scales(p):
                gp.wait_ge(c_ln, 2 * p + 2)
                gp.tensor_tensor(inv[:, 0, :], aggr[:, :, 1], eps[:, :], ALU.add).then_inc(c_inv, 1)
                gp.wait_ge(c_inv, 2 * p + 1)
                gp.tensor_tensor(inv[:, 1, :], inv[:, 0, :], mhalf[:, :], ALU.pow).then_inc(c_inv, 1)
                gp.wait_ge(c_inv, 2 * p + 2)
                centred(p, c_hc)
                gp.wait_ge(c_hc, p + 1)
                wait(gp, c_xt, p)
                gp.tensor_tensor(xn[:, :, :, :], hc[:, :, :].unsqueeze(2).to_broadcast([T, CH, 2, D]),
                                 inv[:, 1, :].unsqueeze(2).unsqueeze(2).to_broadcast([T, CH, 2, D]), ALU.mult)\
                    .then_inc(c_xn, 1)
                gp.tensor_tensor(hn_all[:, ds(p * CH, CH), :], hc[:, :, :], wide(inv[:, 1, :]), ALU.mult)\
                    .then_inc(c_hn, 1)
                gp.wait_ge(c_hn, p + 1)

            def c_result(p):
                gp.wait_ge(c_fin, 3 * p + 3)
                gp.tensor_tensor(inv2[:, 0, :], aggr2[:, :, 1], eps[:, :], ALU.add).then_inc(c_pinv, 1)
                gp.wait_ge(c_pinv, 2 * p + 1)
                gp.tensor_tensor(inv2[:, 1, :], inv2[:, 0, :], mhalf[:, :], ALU.pow).then_inc(c_pinv, 1)
                gp.wait_ge(c_pinv, 2 * p + 2)
                gp.tensor_tensor(yz[:, 0, :, :], yt[:, :, :], wide(aggr2[:, :, 0]), ALU.subtract).then_inc(c_gres, 1)
                gp.wait_ge(c_gres, 4 * p + 1)
                gp.tensor_tensor(yz[:, 1, :, :], yz[:, 0, :, :], wide(inv2[:, 1, :]), ALU.mult).then_inc(c_gres, 1)
                gp.wait_ge(c_gres, 4 * p + 2)
                gp.tensor_tensor(yz[:, 2, :, :], yz[:, 1, :, :], fg_sb[:, :].unsqueeze(1).to_broadcast([T, CH, D]),
                                 ALU.mult).then_inc(c_gres, 1)
                gp.wait_ge(c_gres, 4 * p + 3)
                gp.tensor_tensor(yz[:, 3, :, :], yz[:, 2, :, :], fb_sb[:, :].unsqueeze(1).to_broadcast([T, CH, D]),
                                 ALU.add).then_inc(c_gres, 1)
                gp.wait_ge(c_gres, 4 * p + 4)
                wait(gp, c_out, 16 * p)
                gp.tensor_tensor(res[:, :, :], yz[:, 3, :, :], h_all[:, ds(p * CH, CH), :], ALU.add).then_inc(c_pout, 1)

            def step_c(p, j, old2, old, new, ln):
                if first_step(p):
                    c_scales(0)
                if ln:
                    c_scales(p + 1)
                if old:
                    for g in POOL_GROUPS:
                        gate_group(gp, p - 1, g, 1 - j, c_gatep)
                if old2:
                    c_result(p - 2)

            steps(gp, step_c, BODY_C)

        @block.scalar
        def _(act):
            for dst, src in W_LOADS:
                act.dma_start(full(dst), full(src)).then_inc(ld_w, 16)

            def evac(j, k, i):
                act.wait_ge(a_mm[j], i * STEPS + k + 1)
                ps = bank[j][:, 0:C].rearrange("p (b l) -> p b l", b=2)
                if k < STEPS - 1:
                    act.activation(st_hi[j][:, :, 1:L + 1], ps, ACT.Relu).then_inc(a_hi[j], 2)
                else:
                    act.wait_ge(a_c, i * CHAINS + 1)
                    act.activation(sh_hi[j][0:64, :, 1:L], ps[0:64, :, 0:L - 1], ACT.Relu).then_inc(a_hi[j], 1)
                    act.activation(sh_hi[j][64:128, :, 0:L - 1], ps[64:128, :, L - 2::-1], ACT.Relu)\
                        .then_inc(a_hi[j], 1)

            def round_x(j, i):
                act.wait_ge(a_xin[j], i * 16 + 16)
                wait(act, a_x, (i - 1) * CHAINS + j + 1)
                act.activation(x_rnd[j][:, :], x_raw[j][:, :], ACT.Copy).then_inc(a_rnd, 1)

            def body_a(i, more):
                for k in range(1, STEPS):
                    for j in range(CHAINS):
                        evac(j, k, i)
                    if more and k < CHAINS + 1:
                        round_x(k - 1, i + 1)
                if not more:
                    round_b(0, 0)
                for j in range(0, CHAINS, 2):
                    act.wait_ge(a_c, i * CHAINS + j + 2)
                    act.activation(miu[j][:, :], bank[4 + j][:, 0:C], ACT.Relu).then_inc(a_miu0, 1)
                if more:
                    for j in range(CHAINS):
                        evac(j, 0, i + 1)
                for j in range(0, CHAINS, 2):
                    act.wait_ge(a_t, i * CHAINS + j + 1)
                    act.activation(h_all[:, ds(i * CHAINS * CH + j * CH, CH), :],
                                   bank[4 + j][0:T, :].rearrange("p (c d) -> p c d", c=CH)[:, :, 0:D], ACT.Copy)\
                        .then_inc(a_h, 1)

            def round_b(p, j):
                act.wait_ge(b_xt, p + 1)
                wait(act, b_s1, p)
                act.activation(rnd1[:, :], bank[0][:, 0:C], ACT.Copy).then_inc(b_rnd, 1)
                if first_step(p):
                    act.wait_ge(s_prepg, PREP_G)
                wait(act, b_sc, 16 * (p - 1))
                act.activation(s2[j][0:64, :], bank[0][0:64, 0:C], ACT.Copy).then_inc(b_rnd, 1)

            for j in range(CHAINS):
                round_x(j, 0)
            for j in range(CHAINS):
                evac(j, 0, 0)
            with act.Fori(0, PAIRS // CHAINS - 1) as i:
                body_a(i, True)
            body_a(PAIRS // CHAINS - 1, False)

            def evac_y(p, b):
                act.wait_ge(b_pv, 8 * p + 4 * b + 4)
                wait(act, b_f, p)
                act.activation(y_att[b][:, :], bank[1][:, 0:L], ACT.Copy).then_inc(b_y, 1)

            def step_b(p, j, old2, old, new, ln):
                def exps(v, c):
                    n = 2 * v + c
                    act.wait_ge(b_sc, 16 * (p - 1) + n + 1)
                    wait(act, b_pv, 8 * (p - 1) + v - 1)
                    act.activation(prob[n % 4][:, :, :], bank[5 + n % 3][0:T, 0:C].rearrange("p (h l) -> p h l", h=2),
                                   ACT.Exp).then_inc(b_exp, 1)

                def unit(k):
                    src = bank[2 + k % 3]
                    act.wait_ge(b_pj, 16 * p + k + 1)
                    if is_g(k):
                        wait(act, b_sc, 16 * (p - 1))
                        for a in range(2):
                            last = act.activation(m1[j][64 * a:64 * a + 64, k - 8 + a, :],
                                                  src[64 * a:64 * a + 64, 0:C], ACT.Copy)
                        last.then_inc(b_ev, 1)
                    elif k < 8:
                        wait(act, b_sum, 8 * p + k - 1)
                        act.activation(sq[k % 2][:, :, :], src[0:T, :].rearrange("p (h d) -> p h d", h=H), ACT.Square)\
                            .then_inc(b_ev, 1)
                    else:
                        wait(act, b_pv, 8 * (p - 1))
                        act.activation(u_sb[j][:, (k - 8) // 2, :], src[0:T, :], ACT.Copy).then_inc(b_ev, 1)

                for v in range(8):
                    if new and v == 0 and not first_step(p):
                        round_b(p, j)
                    rest = list(units(v)) if new else []
                    for c in range(2):
                        if old:
                            exps(v, c)
                        if rest:
                            unit(rest.pop(0))
                    if v == 0 and old2:
                        evac_y(p - 2, 1)
                    if v == 4 and old:
                        evac_y(p - 1, 0)
                    for k in rest:
                        unit(k)
                    if new and v == 5:
                        act.wait_ge(b_qt, p + 1)
                        wait(act, b_s2, p)
                        act.activation(rnd2[64:S_ROWS, :], bank[0][64:S_ROWS, 0:C], ACT.Copy).then_inc(b_rnd2, 1)
                    if isinstance(p, int) and p == PAIRS:
                        start_c(v)

            def start_c(v):
                if v == 0:
                    round_c(0)
                else:
                    slot_c(0, 0, False, False, True, True, v - 1)

            def step_b_tail(p, j, old2, old, new, ln):
                if isinstance(p, int) and p == PAIRS + 1:
                    evac_y(p - 2, 1)
                else:
                    step_b(p, j, old2, old, new, ln)

            def round_c(p):
                act.wait_ge(c_xt, p + 1)
                wait(act, c_s1, p)
                act.activation(rnd1[:, :], bank[2][:, 0:C], ACT.Copy).then_inc(c_rnd, 1)

            def slot_c(p, j, old2, old, new, ln, v):
                def relu(g):
                    act.wait_ge(c_up, 16 * (p - 1) + g + 1)
                    wait_gated(act, *((p - 1, g - 4) if g >= 4 else (p - 2, g + 12)))
                    act.activation(relu_sb[g % 4][:, :], bank[4 + g % 4][:, 0:C], ACT.Relu,
                                   bias=b1_sb[:, g:g + 1]).then_inc(c_relu, 1)

                if old2 and v == 2:
                    act.wait_ge(c_dn, 8 * (p - 2) + 8)
                    wait(act, c_f, p - 2)
                    act.activation(y_moe[:, :], bank[1][:, 0:C], ACT.Copy).then_inc(c_y, 1)
                if old:
                    relu(2 * v)
                    relu(2 * v + 1)
                if old and v == 0:
                    act.wait_ge(c_wb, p)
                    for g in (POOL_GROUPS[-1], G - 1):
                        wait_gated(act, p - 3, g)
                    act.activation(wb[1 - j][:, :], bank[0][:, 0:C], ACT.Copy).then_inc(c_wbs, 1)
                if new and v == 0:
                    act.wait_ge(c_lgt, p + 1)
                    wait(act, c_lg, p)
                    act.activation(lgt[:, :], bank[2][0:W_ROWS, 0:C], ACT.Copy).then_inc(c_lgs, 1)
                if new and v == 4:
                    act.wait_ge(c_gate, GATE * p + GATE_D)
                    act.activation(top[:, 7, :], top[:, 6, :], ACT.Exp).then_inc(c_e, 1)
                if ln and v == 6:
                    round_c(p + 1)
                if new and v == 7:
                    act.wait_ge(c_wtt, p + 1)
                    wait(act, c_wt, p)
                    act.activation(rnd2[0:4 * E, :], bank[0][0:4 * E, 0:C], ACT.Copy).then_inc(c_rndw, 1)

            def step_c(p, j, old2, old, new, ln):
                if not first_step(p):
                    for v in range(8):
                        slot_c(p, j, old2, old, new, ln, v)

            steps(act, step_b_tail, BODY_B)
            slot_c(0, 0, False, False, True, True, 7)
            steps(act, step_c, BODY_C)

        @block.vector
        def _(dve):
            count = [0]

            def done(ins):
                count[0] += 1
                ins.then_inc(s_prep, 1)
                dve.wait_ge(s_prep, count[0])

            dve.wait_ge(ld_a, 16 * len(A_LOADS))
            done(dve.tensor_tensor(awt[:, 0, :], aw1_sb[:, :], aw2_sb[:, :], ALU.add))
            done(dve.scalar_tensor_tensor(awt[:, 1, :], cw2_sb[:, :], 2.0, cw1_sb[:, :], ALU.mult, ALU.add))
            done(dve.tensor_copy(awr[:, :, :], awt[:, :, :]))
            mw = c_sb[0:AROWS, C_MW:C_MW + 1]
            dve.scalar_tensor_tensor(aw[:, :], f32(awr[:, 0, :]), mw, awt[:, 0, :], ALU.mult, ALU.add)
            done(dve.scalar_tensor_tensor(cw[:, :], f32(awr[:, 1, :]), mw, awt[:, 1, :], ALU.mult, ALU.add))
            done(dve.tensor_copy(w24_hi[:, :, :], w24_sb[:, :, :]))
            done(dve.tensor_tensor(w24_lo[:, :, :], w24_sb[:, :, :], f32(w24_hi[:, :, :]), ALU.subtract))
            assert count[0] == PREP_A

            def weights():
                dve.tensor_scalar(g2[:, :], gam_sb[:, :], 2.0, None, ALU.mult)
                dve.tensor_scalar(gneg[:, :], gam_sb[:, :], -1.0, None, ALU.mult)
                done(dve.tensor_scalar(cap_lo[:, :], gam_sb[:, :], 0.0, None, ALU.is_lt))
                done(dve.tensor_scalar(cap_hi[:, :], cap_lo[:, :], BIG, 1.0, ALU.mult, ALU.add))
                dve.wait_ge(s_wprod, 1)
                dve.tensor_tensor(wraw[:, 2, :].rearrange("p (h d) -> p h d", h=H),
                                  bank[6][:, :].rearrange("p (h d) -> p h d", h=H),
                                  g2[:, :].unsqueeze(2).to_broadcast([128, H, D]), ALU.mult)
                done(dve.tensor_copy(wraw[:, 3, :], bank[7][:, :]))
                assert count[0] == PREP_W

            def evac(j, k, i):
                dve.wait_ge(a_hi[j], (i * STEPS + k + 1) * 2)
                ps = bank[j][:, 0:C].rearrange("p (b l) -> p b l", b=2)
                if k < STEPS - 1:
                    dve.scalar_tensor_tensor(st_lo[j][:, :, 1:L + 1], ps, 0.0, f32(st_hi[j][:, :, 1:L + 1]),
                                             ALU.max, ALU.subtract).then_inc(a_lo[j], 2)
                else:
                    dve.scalar_tensor_tensor(sh_lo[j][0:64, :, 1:L], ps[0:64, :, 0:L - 1], 0.0,
                                             f32(sh_hi[j][0:64, :, 1:L]), ALU.max, ALU.subtract).then_inc(a_lo[j], 1)
                    dve.scalar_tensor_tensor(sh_lo[j][64:128, :, 0:L - 1], ps[64:128, :, L - 2::-1], 0.0,
                                             f32(sh_hi[j][64:128, :, 0:L - 1]), ALU.max, ALU.subtract)\
                        .then_inc(a_lo[j], 1)

            dve.wait_ge(s_prepg, PREP_GA)
            def stack(j, i):
                dve.wait_ge(a_rnd, i * CHAINS + j + 1)
                if not (isinstance(i, int) and i == 0):
                    dve.wait_ge(a_c, (i - 1) * CHAINS + j + 2)
                dve.scalar_tensor_tensor(x_st[j][0:2 * XROWS, :], f32(x_rnd[j][:, :]),
                                         c_sb[0:2 * XROWS, C_MX:C_MX + 1], x_raw[j][:, :],
                                         ALU.mult, ALU.add).then_inc(a_x, 1)

            def body_a(i, more):
                for k in range(1, STEPS):
                    for j in range(CHAINS):
                        evac(j, k, i)
                    if not more and k == 4:
                        dve.wait_ge(a_h, CHAINS + 1)
                        norm(0, b_ln)
                for j in range(CHAINS):
                    if more:
                        stack(j, i + 1)
                    elif j == 0:
                        stack_b(0, 0)
                    if j % 2:
                        dve.wait_ge(a_c, i * CHAINS + j + 2)
                        dve.tensor_scalar(miu[j][:, :], bank[4 + j][:, 0:C], 0.0, None, ALU.max).then_inc(a_miu1, 1)
                if more:
                    for j in range(CHAINS):
                        evac(j, 0, i + 1)
                for j in range(1, CHAINS, 2):
                    dve.wait_ge(a_t, i * CHAINS + j + 1)
                    dve.tensor_copy(h_all[:, ds(i * CHAINS * CH + j * CH, CH), :],
                                    bank[4 + j][0:T, :].rearrange("p (c d) -> p c d", c=CH)[:, :, 0:D]).then_inc(a_h, 1)

            def norm(p, s_ln):
                norm_stats(p, s_ln)
                norm_aggr(p, s_ln)

            def norm_stats(p, s_ln):
                for c in range(CH):
                    last = dve.bn_stats(stats[:, c, :], h_all[:, ds(p * CH + c, 1), :])
                last.then_inc(s_ln, 1)

            def norm_aggr(p, s_ln):
                dve.wait_ge(s_ln, 2 * p + 1)
                wait(dve, b_xn if s_ln is b_ln else c_hn, p)
                dve.memset(spare[:, :], 0.0)
                for c in range(CH):
                    last = dve.bn_aggr(aggr[:, c, :], stats[:, c, :])
                last.then_inc(s_ln, 1)

            def stack_b(p, j):
                dve.wait_ge(b_rnd, 2 * p + 2)
                wait(dve, b_sc, 16 * (p - 1))
                dve.scalar_tensor_tensor(s1[j][:, :], f32(rnd1[:, :]), c_sb[:, C_MS1:C_MS1 + 1],
                                         bank[0][:, 0:C], ALU.mult, ALU.add).then_inc(b_s1, 1)

            for j in range(CHAINS):
                stack(j, 0)
            for j in range(CHAINS):
                evac(j, 0, 0)
            weights()
            with dve.Fori(0, PAIRS // CHAINS - 1) as i:
                body_a(i, True)
            body_a(PAIRS // CHAINS - 1, False)

            def residual(p, k):
                rows = h_all[:, ds(p * CH, CH), :]
                part = bank[0][0:T, :].rearrange("p (c a d) -> p c a d", c=CH, a=2)[:, :, k, :]
                if k == 0:
                    dve.wait_ge(b_f, p + 1)
                    dve.tensor_tensor(z2[:, :, :], part, rows, ALU.add).then_inc(b_half, 1)
                else:
                    dve.wait_ge(b_half, p + 1)
                    dve.tensor_tensor(rows, part, z2[:, :, :], ALU.add).then_inc(b_res, 1)

            def step_b(p, j, old2, old, new, ln):
                def caps(v, c):
                    n = 2 * v + c
                    dve.wait_ge(b_exp, 16 * (p - 1) + n + 1)
                    for hh in range(2):
                        h = (2 * v + hh) % H
                        part = prob[n % 4][:, hh, :]
                        last = dve.tensor_scalar(part, part, cap_hi[0:T, h:h + 1], cap_lo[0:T, h:h + 1],
                                                 ALU.min, ALU.max)
                    last.then_inc(b_cap, 1)

                def unit(k):
                    if 2 <= k < 10:
                        n = k - 2
                        if n == 0:
                            wait(dve, b_qkw, 2 * p)
                        dve.wait_ge(b_sum, 8 * p + n + 1)
                        dve.tensor_reduce(qk[:, n // 2, n % 2, :], sq2[n % 2][:, :, :], AX.X, ALU.add)\
                            .then_inc(b_red, 1)
                    if is_g(k):
                        dve.wait_ge(b_ev, 16 * p + k + 1)
                        for a in range(2):
                            rows, h = slice(64 * a, 64 * a + 64), k - 8 + a
                            last = dve.tensor_tensor(m2[j][0:64, h, :], bank[2 + k % 3][rows, 0:C],
                                                     f32(m1[j][rows, h, :]), ALU.subtract)
                        last.then_inc(b_gl, 1)

                if isinstance(p, int) and p == PAIRS - 1:
                    wait(dve, b_xn, PAIRS)
                    norm(0, c_ln)
                for v in range(8):
                    if new and v == 0 and not first_step(p):
                        stack_b(p, j)
                    rest = list(units(v)) if new else []
                    for c in range(2):
                        if old:
                            caps(v, c)
                        if old2 and v == 3 and c == 0:
                            residual(p - 2, 1)
                        if rest:
                            unit(rest.pop(0))
                    for k in rest:
                        unit(k)
                    if v == 2 and old2:
                        residual(p - 2, 0)
                    if new and v == 5:
                        dve.wait_ge(b_rnd2, p + 1)
                        dve.scalar_tensor_tensor(s2[j][64:S_ROWS, :], f32(rnd2[64:S_ROWS, :]),
                                                 c_sb[64:S_ROWS, C_MS2:C_MS2 + 1], bank[0][64:S_ROWS, 0:C],
                                                 ALU.mult, ALU.add).then_inc(b_s2, 1)
                    if ln and v == 0:
                        norm_stats(p + 1, b_ln)
                    if ln and v == 1:
                        norm_aggr(p + 1, b_ln)
                    if isinstance(p, int) and p == PAIRS:
                        start_c(v)

            def start_c(v):
                if v == 0:
                    stack_c(0, 0)
                elif v < 7:
                    for g in (2 * v - 2, 2 * v - 1):
                        group_c(0, 0, False, False, True, True, g)

            def step_b_tail(p, j, old2, old, new, ln):
                if isinstance(p, int) and p == PAIRS + 1:
                    pass
                else:
                    step_b(p, j, old2, old, new, ln)

            def gate_step(p, n):
                def done(ins):
                    ins.then_inc(c_gate, 1)

                def wide(t):
                    return t.unsqueeze(2).to_broadcast([T, CH, E])

                dsc = desc[:, :].unsqueeze(1).to_broadcast([T, CH, E])
                if n == LOGITS:
                    dve.wait_ge(c_lg, p + 1)
                elif n == 0:
                    dve.wait_ge(c_lsum, p + 1)
                else:
                    dve.wait_ge(c_gate, GATE * p + (n - 1 if n == GATE_D else n))
                parts = bank[3][0:T, 0:CH * W_ROWS].rearrange("p (c e) -> p c e", c=CH)
                if n == LOGITS:
                    dve.tensor_tensor(lg[:, 7, :, :], parts[:, :, 0:E], gb_sb[:, :].unsqueeze(1).to_broadcast([T, CH, E]),
                                      ALU.add).then_inc(c_lsum, 1)
                if n == 0:
                    done(dve.tensor_tensor(lg[:, 0, :, :], parts[:, :, GW_LO:GW_LO + E], lg[:, 7, :, :], ALU.add))
                k, src = (0, lg[:, 0, :, :]) if n < 7 else (1, lg[:, 3, :, :])
                if n in (1, 7):
                    done(dve.tensor_reduce(top[:, 2 * k, :], src, AX.X, ALU.max))
                if n in (2, 9):
                    done(dve.tensor_tensor(lg[:, 1, :, :], src, wide(top[:, 2 * k, :]), ALU.is_equal))
                if n in (3, 10):
                    done(dve.tensor_tensor(lg[:, 5, :, :], lg[:, 1, :, :], dsc, ALU.mult))
                if n in (4, 11):
                    done(dve.tensor_reduce(top[:, 2 * k + 1, :], lg[:, 5, :, :], AX.X, ALU.max))
                if n in (5, 12):
                    done(dve.tensor_tensor(lg[:, 2 + 2 * k, :, :], lg[:, 5, :, :], wide(top[:, 2 * k + 1, :]),
                                           ALU.is_equal))
                if n == 6:
                    done(dve.scalar_tensor_tensor(lg[:, 3, :, :], lg[:, 2, :, :], -BIG, lg[:, 0, :, :],
                                                  ALU.mult, ALU.add))
                if n == 8:
                    done(dve.tensor_tensor(top[:, 6, :], top[:, 2, :], top[:, 0, :], ALU.subtract))
                if n == 13:
                    dve.wait_ge(c_e, p + 1)
                    done(dve.tensor_scalar(top[:, 8, :], top[:, 7, :], 1.0, None, ALU.add))
                if n == 14:
                    done(dve.reciprocal(top[:, 9, :], top[:, 8, :]))
                if n == 15:
                    done(dve.tensor_tensor(top[:, 10, :], top[:, 9, :], top[:, 7, :], ALU.mult))
                if n == 16:
                    dve.tensor_tensor(lg[:, 5, :, :], lg[:, 2, :, :], wide(top[:, 9, :]), ALU.mult)
                    done(dve.tensor_tensor(lg[:, 6, :, :], lg[:, 4, :, :], wide(top[:, 10, :]), ALU.mult))
                if n == 17:
                    wait(dve, c_wtt, p)
                    first, second = (lg[:, k, :, :].unsqueeze(2).to_broadcast([T, CH, 4, E]) for k in (5, 6))
                    done(dve.tensor_tensor(wtok[:, :, 0:4 * E].rearrange("p c (a e) -> p c a e", a=4),
                                           first, second, ALU.add))

            def result(p, n):
                sums = bank[3][0:T, :].rearrange("p (c a d) -> p c a d", c=CH, a=2)
                if n == 0:
                    dve.wait_ge(c_f, p + 1)
                    dve.tensor_tensor(yt2[:, :, :], sums[:, :, 0, :], hn_all[:, ds(p * CH, CH), :], ALU.add)\
                        .then_inc(c_half, 1)
                if n == 1:
                    dve.wait_ge(c_half, p + 1)
                    wait(dve, c_gres, 4 * p - 3)
                    dve.tensor_tensor(yt[:, :, :], sums[:, :, 1, :], yt2[:, :, :], ALU.add).then_inc(c_fin, 1)
                if n == 2:
                    dve.wait_ge(c_fin, 3 * p + 1)
                    for c in range(CH):
                        last = dve.bn_stats(stats2[:, c, :], yt[:, c, :])
                    last.then_inc(c_fin, 1)
                if n == 3:
                    dve.wait_ge(c_fin, 3 * p + 2)
                    dve.memset(spare[:, :], 0.0)
                    for c in range(CH):
                        last = dve.bn_aggr(aggr2[:, c, :], stats2[:, c, :])
                    last.then_inc(c_fin, 1)
            def stack_c(p, j):
                dve.wait_ge(c_rnd, p + 1)
                wait(dve, c_up, 16 * (p - 1))
                dve.scalar_tensor_tensor(s1[j][:, :], f32(rnd1[:, :]), c_sb[:, C_MS1:C_MS1 + 1],
                                         bank[2][:, 0:C], ALU.mult, ALU.add).then_inc(c_s1, 1)

            GATE_AT = {2: (LOGITS, 0), 3: (1, 2, 3), 4: (4, 5, 6), 5: (7, 8, 9), 6: (10, 11), 7: (12,), 8: (13, 14),
                       9: (15, 16), 10: (17,)}
            RESULT_AT = {7: 0, 8: 1, 9: 2, 10: 3}

            def group_c(p, j, old2, old, new, ln, g):
                if old and g not in POOL_GROUPS:
                    gate_group(dve, p - 1, g, 1 - j, c_gated)
                if ln and g == 0:
                    norm_stats(p + 1, c_ln)
                if ln and g == 1:
                    norm_aggr(p + 1, c_ln)
                if isinstance(p, int) and p == 1 and g in (3, 4):
                    residual(PAIRS - 1, g - 3)
                at = GATE_AT.get(g, ()) if new else ()
                for n in at[:1]:
                    gate_step(p, n)
                if old2 and g in RESULT_AT:
                    result(p - 2, RESULT_AT[g])
                for n in at[1:]:
                    gate_step(p, n)
                if new and g == 13:
                    dve.wait_ge(c_rndw, p + 1)
                    wait(dve, c_dn, 8 * (p - 1))
                    dve.scalar_tensor_tensor(wt[j][:, :], f32(rnd2[0:4 * E, :]), c_sb[0:4 * E, C_MG:C_MG + 1],
                                             bank[0][0:4 * E, 0:C], ALU.mult, ALU.add).then_inc(c_wt, 1)
                if ln and g == 14:
                    stack_c(p + 1, 1 - j)

            def step_c(p, j, old2, old, new, ln):
                if not first_step(p):
                    for g in range(16):
                        group_c(p, j, old2, old, new, ln, g)

            steps(dve, step_b_tail, BODY_B)
            for g in range(12, 16):
                group_c(0, 0, False, False, True, True, g)
            steps(dve, step_c, BODY_C)

        @block.tensor
        def _(pe):
            pe.wait_ge(ld_w, 16 * len(W_LOADS))
            for h in range(H):
                pe.matmul(bank[6][:, h * D:(h + 1) * D], wqv_sb[0:64, h, :], wko_sb[0:64, h, :], start=True, stop=True)
                last = pe.matmul(bank[7][:, h * D:(h + 1) * D], wqv_sb[64:128, h, :], wko_sb[64:128, h, :],
                                 start=True, stop=True)
            last.then_inc(s_wprod, 1)
            pe.wait_ge(s_prep, PREP_A)
            pe.wait_ge(s_prepg, PREP_GA)

            def three(dst, w, hi, lo):
                dst = dst[:, 0:C].rearrange("p (b l) -> p b l", b=2)
                pe.matmul(dst, w24_hi[:, w, :], hi, start=False, stop=False)
                pe.matmul(dst, w24_lo[:, w, :], hi, start=False, stop=False)
                return pe.matmul(dst, w24_hi[:, w, :], lo, start=False, stop=True)

            def inputs(j, i):
                pe.wait_ge(a_x, i * CHAINS + j + 1)
                pe.matmul(bank[j][:, 0:C], aw[:, :], x_st[j][:, :], start=True, stop=True).then_inc(a_mm[j], 1)

            def body_a(i, more):
                for k in range(1, STEPS):
                    for j in range(CHAINS):
                        pe.wait_ge(a_lo[j], (i * STEPS + k) * 2)
                        pe.matmul(bank[j][:, 0:C], aw[:, :], x_st[j][:, :], start=True, stop=False)
                        three(bank[j], 0, st_hi[j][:, :, 0:L], st_lo[j][:, :, 0:L]).then_inc(a_mm[j], 1)
                pe.wait_ge(s_prep, PREP_W)
                for j in range(CHAINS):
                    pe.wait_ge(a_lo[j], (i * STEPS + STEPS) * 2)
                    pe.wait_ge(a_h, i * CHAINS + 1)
                    pe.matmul(bank[4 + j][:, 0:C], cw[:, :], x_st[j][:, :], start=True, stop=False)
                    three(bank[4 + j], 1, sh_hi[j][:, :, :], sh_lo[j][:, :, :]).then_inc(a_c, 1)
                    if not more and j == 0:
                        tokens_b(0)
                if more:
                    for j in range(CHAINS):
                        inputs(j, i + 1)
                for j in range(CHAINS):
                    pe.wait_ge((a_miu0, a_miu1)[j % 2], i * 2 + j // 2 + 1)
                    for c in range(CH):
                        last = pe.transpose(bank[4 + j][0:T, c * 128:(c + 1) * 128], miu[j][:, c * T:(c + 1) * T], ident)
                    last.then_inc(a_t, 1)

            def tokens_b(p):
                pe.wait_ge(b_xn, p + 1)
                wait(pe, b_s2, p)
                for c in range(CH):
                    last = pe.transpose(bank[0][:, c * T:(c + 1) * T],
                                        xn[:, c, :, :].rearrange("p a d -> p (a d)"), ident[0:T, 0:T])
                last.then_inc(b_xt, 1)

            for j in range(CHAINS):
                inputs(j, 0)
            with pe.Fori(0, PAIRS // CHAINS - 1) as i:
                body_a(i, True)
            body_a(PAIRS // CHAINS - 1, False)

            def products(p, v, jj, hh):
                b = v // 4
                if hh == 0:
                    pe.wait_ge(b_cap, 16 * p + 2 * v + 2)
                    if v == 0:
                        pe.wait_ge(b_ev, 16 * (p + 1))
                    if v % 4 == 0:
                        wait(pe, b_y, 2 * p + b)
                h = (2 * v + hh) % H
                for c in range(2):
                    last = pe.matmul(bank[1][64 * c:64 * c + 64, 0:L], u_sb[jj][:, 2 * b + c, h * D:(h + 1) * D],
                                     prob[(2 * v + c) % 4][:, hh, :], start=h == 0, stop=h == H - 1)
                if hh == 1:
                    last.then_inc(b_pv, 1)

            def fold_b(p):
                pe.wait_ge(b_y, 2 * p + 2)
                for c in range(CH):
                    last = pe.transpose(bank[0][0:T, c * 128:(c + 1) * 128],
                                        y_att[c // 2][:, (c % 2) * T:(c % 2 + 1) * T], ident)
                last.then_inc(b_f, 1)

            def step_b(p, j, old2, old, new, ln):
                o = 1 - j

                def scores(v, c):
                    b, hp, n = v // 4, v % 4, 2 * v + c
                    wait(pe, b_exp, 16 * (p - 1) + (n - 2 if n > 2 else (0, -2, -1)[n]))
                    if n < 8 and c == 0:
                        pe.wait_ge(b_gl, 4 * (p - 1) + hp + 1)
                        pe.wait_ge(b_dup[hp], 32 * p)
                    cols = slice((2 * b + c) * T, (2 * b + c + 1) * T)
                    ps = bank[5 + n % 3][0:T, 0:C].rearrange("p (h l) -> p h l", h=2)
                    pe.matmul(ps, s1[o][:, cols], m1[o][:, 2 * hp:2 * hp + 2, b * L:(b + 1) * L],
                              start=True, stop=False)
                    pe.matmul(ps, s2[o][:, cols], m2[o][:, 2 * hp:2 * hp + 2, b * L:(b + 1) * L],
                              start=False, stop=True).then_inc(b_sc, 1)

                def unit(k):
                    dst = bank[2 + k % 3]
                    if k < 3:
                        wait(pe, b_ev, 16 * p)
                        wait(pe, b_gl, 4 * p)
                        if first_step(p) and k == 2:
                            pe.wait_ge(a_h, PAIRS + 1)
                    elif is_g(k - 3):
                        pe.wait_ge(b_gl, 4 * p + (k - 11) // 2 + 1)
                    else:
                        pe.wait_ge(b_ev, 16 * p + k - 2)
                    if k == 0:
                        pe.wait_ge(b_s1, p + 1)
                    c, q = (k // 2, k % 2) if k < 8 else ((k - 8) // 2, 2)
                    for hi_lo, first in ((0, True), (1, False)):
                        if not is_g(k):
                            w = (wqku_hi, wqku_lo)[hi_lo]
                            last = pe.matmul(dst[0:T, :], s1[j][:, c * T:(c + 1) * T], w[:, q, :],
                                             start=first, stop=not first)
                        else:
                            w = (wg_hi, wg_lo)[hi_lo]
                            last = pe.matmul(dst[:, 0:C], w[:, (k - 8) * 64:(k - 6) * 64],
                                             s1[j][:, :], start=first, stop=not first)
                    last.then_inc(b_pj, 1)

                for v in range(8):
                    if new and v == 0 and not first_step(p):
                        tokens_b(p)
                    if old and v == 0:
                        pe.wait_ge(b_row, 32 * p)
                    rest = list(units(v)) if new else []
                    for c in range(2):
                        if old:
                            scores(v, c)
                        if rest:
                            unit(rest.pop(0))
                    for k in rest:
                        unit(k)
                    for hh in range(2):
                        if v == 0 and old2:
                            products(p - 2, 7, j, hh)
                        if v > 0 and old:
                            products(p - 1, v - 1, o, hh)
                    if old2 and v == 1:
                        if new:
                            pe.wait_ge(b_s1, p + 1)
                        fold_b(p - 2)
                    if new and v == 5:
                        pe.wait_ge(b_qkw, 2 * p + 2)
                        wait(pe, b_res, p - 1)
                        for c in range(CH):
                            last = pe.transpose(bank[0][0:S_ROWS, c * T:(c + 1) * T], qkw[:, c, :], ident[0:T, 0:T])
                        last.then_inc(b_qt, 1)
                    if isinstance(p, int) and p == PAIRS:
                        start_c(v)

            def start_c(v):
                if v == 0:
                    pe.wait_ge(b_ev, 16 * PAIRS)
                    tokens_c(0)
                else:
                    slot_c(0, 0, False, False, True, True, v - 1)

            def step_b_tail(p, j, old2, old, new, ln):
                if isinstance(p, int) and p == PAIRS + 1:
                    products(p - 2, 7, j, 0)
                    products(p - 2, 7, j, 1)
                else:
                    step_b(p, j, old2, old, new, ln)

            def down(p, v, jj):
                y = bank[1]
                if v == 0:
                    wait(pe, c_y, p)
                    pe.matmul(y[:, 0:C], b2_st[:, :], wt[jj][:, :], start=True, stop=False, skip_group_check=True)
                for g in (2 * v, 2 * v + 1):
                    wait_gated(pe, p, g)
                for k in range(2):
                    g = 2 * v + k
                    last = pe.matmul(y[64 * k:64 * k + 64, 0:C], w2_sb[:, g, :], gated[g % 8][:, :],
                                     start=False, stop=v == 7, skip_group_check=True)
                last.then_inc(c_dn, 1)

            def tokens_c(p):
                pe.wait_ge(c_xn, p + 1)
                wait(pe, c_lgs, p)
                for c in range(CH):
                    last = pe.transpose(bank[2][:, c * T:(c + 1) * T],
                                        xn[:, c, :, :].rearrange("p a d -> p (a d)"), ident[0:T, 0:T])
                last.then_inc(c_xt, 1)

            def slot_c(p, j, old2, old, new, ln, v):
                o = 1 - j

                def up(g):
                    wait(pe, c_relu, 16 * (p - 1) + g - 3)
                    for w, first in ((w1_hi, True), (w1_lo, False)):
                        last = pe.matmul(bank[4 + g % 4][:, 0:C], w[:, g, :], s1[o][:, :], start=first, stop=not first)
                    last.then_inc(c_up, 1)

                if old:
                    up(2 * v)
                    up(2 * v + 1)
                if old and v == 0:
                    pe.wait_ge(c_wt, p)
                    pe.matmul(bank[0][:, 0:C], sel[:, :], wt[o][0:2 * E, :], start=True, stop=True).then_inc(c_wb, 1)
                if isinstance(p, int) and p == 1 and v == 1:
                    pe.wait_ge(c_wbs, 1)
                    fold_b(PAIRS - 1)
                if new and v == 7:
                    pe.wait_ge(c_gate, GATE * (p + 1))
                    wait(pe, c_wbs, p)
                    pe.wait_ge(b_res, PAIRS if not first_step(p) else PAIRS - 1)
                    for c in range(CH):
                        last = pe.transpose(bank[0][0:W_ROWS, c * T:(c + 1) * T], wtok[:, c, :], ident[0:T, 0:T])
                    last.then_inc(c_wtt, 1)
                if v < 2 and old2:
                    down(p - 2, v + 6, j)
                if v >= 2 and old:
                    down(p - 1, v - 2, o)
                if new and v == 0:
                    pe.wait_ge(c_s1, p + 1)
                    pe.matmul(bank[2][0:W_ROWS, 0:C], gw_st[:, :], s1[j][:, :], start=True, stop=True).then_inc(c_lgt, 1)
                if new and v == 1:
                    pe.wait_ge(c_lgs, p + 1)
                    wait(pe, c_fin, 3 * (p - 3) + 1)
                    for c in range(CH):
                        last = pe.transpose(bank[3][0:T, c * W_ROWS:(c + 1) * W_ROWS], lgt[:, c * T:(c + 1) * T],
                                            ident[0:W_ROWS, 0:W_ROWS])
                    last.then_inc(c_lg, 1)
                if old2 and v == 3:
                    pe.wait_ge(c_y, p - 1)
                    if new:
                        pe.wait_ge(c_gate, GATE * p + 1)
                    for c in range(CH):
                        last = pe.transpose(bank[3][0:T, c * 128:(c + 1) * 128], y_moe[:, c * T:(c + 1) * T], ident)
                    last.then_inc(c_f, 1)
                if ln and v == 6:
                    tokens_c(p + 1)

            def step_c(p, j, old2, old, new, ln):
                if not first_step(p):
                    for v in range(8):
                        slot_c(p, j, old2, old, new, ln, v)

            pe.wait_ge(s_prepg, PREP_G)
            steps(pe, step_b_tail, BODY_B)
            slot_c(0, 0, False, False, True, True, 7)
            steps(pe, step_c, BODY_C)


PREP_A = 6
PREP_W = 9
PREP_GA = 7 * CHAINS
PREP_G = PREP_GA + 26
GATE_D = 9
POOL_GROUPS = (6, 8)
LOGITS = -1
GATE = 18


def kernel(**inputs):
    import concourse.bacc as bacc
    from concourse.bass_utils import run_bass_kernel_spmd

    def a(name):
        return np.asarray(inputs[name])

    def rows(x, n):
        return np.broadcast_to(x[None], (n,) + x.shape)

    def stacked(w, rev_left, rev_right, fwd_left, fwd_right, bias):
        o = np.zeros((AROWS, 128), np.float32)
        for g in range(4):
            f = slice(g * D_IN, (g + 1) * D_IN)
            r = slice(XROWS + g * D_IN, XROWS + (g + 1) * D_IN)
            for half, fwd, rev in ((0, fwd_left, rev_left), (1, fwd_right, rev_right)):
                cols = slice(half * D, half * D + D)
                if fwd:
                    o[f, cols] = w.T
                if rev:
                    o[r, cols] = w.T
        o[AROWS - 2:, :] = np.concatenate([bias, bias])
        return o

    def bias_rows(b):
        o = np.zeros((AROWS, 128), np.float32)
        o[AROWS - 2:, :] = np.concatenate([b, b])
        return o

    x = a("x").reshape(PAIRS, 2, D_IN, L).transpose(0, 2, 1, 3)
    xr = np.concatenate([np.tile(x, (1, 4, 1, 1)), np.tile(x[..., ::-1], (1, 4, 1, 1))], axis=1)
    W2T, W4T = a("L0_tok_W2").T, a("L0_tok_W4").T
    w2bd = np.zeros((128, 128), np.float32)
    w2bd[:D, :D] = W2T
    w2bd[D:, D:] = W2T
    w_q, w_k, w_v = a("L0_attn_W_q"), a("L0_attn_W_k"), a("L0_attn_W_v")
    qT, kT, vT = (w.transpose(2, 0, 1) for w in (w_q, w_k, w_v))
    oT = a("L0_attn_W_o").reshape(D, H, D).transpose(2, 1, 0)
    b2 = np.zeros((4 * E, 128), np.float32)
    b2[:, 0:D] = np.tile(a("L0_ffn_b2"), (4, 1))
    gate_w = np.zeros((128, W_ROWS), np.float32)
    gate_w[:, 0:E] = gate_w[:, GW_LO:GW_LO + E] = np.tile(a("L0_ffn_gate_w"), (2, 1))
    w1 = a("L0_ffn_w1").reshape(E, D, G, R)
    arrays = {
        "cst": constants(),
        "xr": xr.reshape(PAIRS, 2 * XROWS, C),
        "aw1": stacked(a("L0_tok_W1"), False, True, True, False, a("L0_tok_b1")),
        "aw2": bias_rows(a("L0_tok_b2")),
        "cw1": stacked(a("L0_tok_W3"), False, False, True, True, a("L0_tok_b3")),
        "cw2": bias_rows(a("L0_tok_b4")),
        "w24": np.stack([w2bd, np.tile(W4T, (2, 2))], axis=1),
        "wqT": np.concatenate([qT, qT], axis=2),
        "wkT": kT,
        "wvT": np.concatenate([vT, vT], axis=2),
        "woT": oT,
        "wq": np.tile(w_q.transpose(1, 0, 2).reshape(D, H * D), (2, 1)),
        "wk": np.tile(w_k.transpose(1, 0, 2).reshape(D, H * D), (2, 1)),
        "gam": rows(a("L0_attn_gamma").reshape(H), 128),
        "lns": rows(a("L0_attn_ln_scale"), T),
        "gw": gate_w,
        "gb": rows(a("L0_ffn_gate_b"), T),
        "w1": np.tile(w1.transpose(1, 2, 0, 3).reshape(D, G, 128), (2, 1, 1)),
        "b1": a("L0_ffn_b1").reshape(E, G, R).transpose(0, 2, 1).reshape(128, G),
        "w2": a("L0_ffn_w2").reshape(E, G, R, D).transpose(0, 2, 1, 3).reshape(128, G, D),
        "b2": b2,
        "fg": rows(a("L0_ffn_gamma"), T),
        "fb": rows(a("L0_ffn_beta"), T),
    }
    nc = bacc.Bacc("TRN2", target_bir_lowering=False, num_devices=1)
    ins, args = {}, {}
    for name, v in arrays.items():
        v = np.ascontiguousarray(v)
        ins[f"in_{name}"] = v
        args[name] = nc.dram_tensor(f"in_{name}", v.shape, mybir.dt.from_np(v.dtype), kind="ExternalInput").ap()
    out = nc.dram_tensor("out", (B, L, D), F32, kind="ExternalOutput").ap()
    build(nc, **args, out=out)
    r = run_bass_kernel_spmd(nc, [ins], core_ids=[0])
    return r.results[0]["out"]
```
